# Optimizing a Trainium2 kernel written in Bass

```python
import numpy as np
import jax
import jax.numpy as jnp

def _softmax(x, axis=-1):
    return jax.nn.softmax(x, axis=axis)

def _gelu(x):
    return jax.nn.gelu(x, approximate=True)

def _silu(x):
    return jax.nn.silu(x)

def _sigmoid(x):
    return jax.nn.sigmoid(x)

def _layernorm(x, axis=-1, eps=1e-05):
    m = jnp.mean(x, axis=axis, keepdims=True)
    v = jnp.var(x, axis=axis, keepdims=True)
    return (x - m) / jnp.sqrt(v + eps)

def _scatter_add(tgt, idx, src, axis=0):
    return tgt.at[idx].add(src)

def _segment_sum(src, seg, n):
    return jax.ops.segment_sum(src, seg, n)
kernel_name = 'mk_macaron_d1_jaxref_r8_f62fdc'

def setup_inputs(seed: int=0):
    np.random.seed(seed)
    _w = jnp.asarray

    def _L0_attn_setup():
        import jax, jax.numpy as jnp
        import numpy as np
        import math
        D_MODEL = 128
        D_STATE = 16
        D_CONV = 4
        EXPAND = 2
        D_INNER = EXPAND * D_MODEL
        D_HALF = D_INNER // 2
        DT_RANK = math.ceil(D_MODEL / 16)
        BATCH = 4
        SEQLEN = 128

        def _dwconv_same(x, K, b):
            k = K.shape[-1]
            y = jax.lax.conv_general_dilated(x, K, window_strides=(1,), padding=[((k - 1) // 2, k // 2)], dimension_numbers=('NCH', 'OIH', 'NCH'), feature_group_count=x.shape[1])
            return y + b[None, :, None]

        def _selective_scan(u, delta, A, Bm, Cm, Dp):
            dA = jnp.exp(jnp.einsum('bdl,dn->lbdn', delta, A))
            dBu = jnp.einsum('bdl,bnl,bdl->lbdn', delta, Bm, u)
            Ct = jnp.transpose(Cm, (2, 0, 1))
            h0 = jnp.zeros(dA.shape[1:], dA.dtype)

            def step(h, inp):
                dA_t, dBu_t, C_t = inp
                h = dA_t * h + dBu_t
                return (h, jnp.einsum('bdn,bn->bd', h, C_t))
            _, ys = jax.lax.scan(step, h0, (dA, dBu, Ct))
            y = jnp.transpose(ys, (1, 2, 0))
            return y + u * Dp[None, :, None]
        key = jax.random.key(seed)
        ks = jax.random.split(key, 10)

        def s(k, shape, scale):
            return jax.random.normal(k, shape, jnp.float32) * scale
        hidden_states = jax.random.normal(ks[0], (BATCH, SEQLEN, D_MODEL), jnp.float32)
        W_in = s(ks[1], (D_MODEL, D_INNER), D_MODEL ** (-0.5))
        W_xproj = s(ks[2], (D_HALF, DT_RANK + 2 * D_STATE), D_HALF ** (-0.5))
        dt_init_std = DT_RANK ** (-0.5)
        W_dt = jax.random.uniform(ks[3], (DT_RANK, D_HALF), jnp.float32, -dt_init_std, dt_init_std)
        dt = jnp.exp(jax.random.uniform(ks[4], (D_HALF,), jnp.float32, math.log(0.001), math.log(0.1)))
        dt = jnp.clip(dt, 0.0001, None)
        b_dt = dt + jnp.log(-jnp.expm1(-dt))
        A_log = jnp.log(jnp.tile(jnp.arange(1, D_STATE + 1, dtype=jnp.float32)[None, :], (D_HALF, 1)))
        D = jnp.ones((D_HALF,), jnp.float32)
        W_out = s(ks[5], (D_INNER, D_MODEL), D_INNER ** (-0.5))
        K_x = s(ks[6], (D_HALF, 1, D_CONV), 0.3)
        b_x = jnp.zeros((D_HALF,), jnp.float32)
        K_z = s(ks[7], (D_HALF, 1, D_CONV), 0.3)
        b_z = jnp.zeros((D_HALF,), jnp.float32)
        return dict(hidden_states=hidden_states, W_in=W_in, W_xproj=W_xproj, W_dt=W_dt, b_dt=b_dt, A_log=A_log, D=D, W_out=W_out, K_x=K_x, b_x=b_x, K_z=K_z, b_z=b_z)
    _L0_attn_in = _L0_attn_setup()

    def _L0_ffn_setup():
        import jax, jax.numpy as jnp
        import numpy as np
        B, S, D = (1, 256, 128)
        E, F = (16, 128)
        NG, TKG, K = (4, 2, 4)
        NSH = 2
        SCALE = 2.5
        STD = 0.02
        EPG = E // NG

        def _route(x_flat, router_w, bias):
            logits = x_flat.astype(jnp.float32) @ router_w.T
            scores = jax.nn.sigmoid(logits)
            s = scores + bias[None, :]
            sg = s.reshape(-1, NG, EPG)
            group_score = jax.lax.top_k(sg, 2)[0].sum(-1)
            gidx = jax.lax.top_k(group_score, TKG)[1]
            gmask = jnp.sum(jax.nn.one_hot(gidx, NG, dtype=jnp.float32), axis=1) > 0
            emask = jnp.repeat(gmask, EPG, axis=1)
            masked = jnp.where(emask, s, -1.0)
            topk_idx = jax.lax.top_k(masked, K)[1]
            tw = jnp.take_along_axis(scores, topk_idx, axis=1)
            tw = tw / (tw.sum(-1, keepdims=True) + 1e-20)
            tw = tw * SCALE
            return (topk_idx, tw)
        key = jax.random.key(seed)
        ks = jax.random.split(key, 8)
        return {'hidden_states': jax.random.normal(ks[0], (B, S, D), jnp.float32), 'router_w': jax.random.normal(ks[1], (E, D), jnp.float32) * STD, 'bias': jnp.zeros((E,), jnp.float32), 'gate_w': jax.random.normal(ks[2], (E, D, F), jnp.float32) * STD, 'up_w': jax.random.normal(ks[3], (E, D, F), jnp.float32) * STD, 'down_w': jax.random.normal(ks[4], (E, F, D), jnp.float32) * STD, 'sh_gate_w': jax.random.normal(ks[5], (D, NSH * F), jnp.float32) * STD, 'sh_up_w': jax.random.normal(ks[6], (D, NSH * F), jnp.float32) * STD, 'sh_down_w': jax.random.normal(ks[7], (NSH * F, D), jnp.float32) * STD}
    _L0_ffn_in = _L0_ffn_setup()
    _d = {'L0_attn_hidden_states': _L0_attn_in['hidden_states'], 'L0_attn_W_in': _L0_attn_in['W_in'], 'L0_attn_W_xproj': _L0_attn_in['W_xproj'], 'L0_attn_W_dt': _L0_attn_in['W_dt'], 'L0_attn_b_dt': _L0_attn_in['b_dt'], 'L0_attn_A_log': _L0_attn_in['A_log'], 'L0_attn_D': _L0_attn_in['D'], 'L0_attn_W_out': _L0_attn_in['W_out'], 'L0_attn_K_x': _L0_attn_in['K_x'], 'L0_attn_b_x': _L0_attn_in['b_x'], 'L0_attn_K_z': _L0_attn_in['K_z'], 'L0_attn_b_z': _L0_attn_in['b_z'], 'L0_ffn_router_w': _L0_ffn_in['router_w'], 'L0_ffn_bias': _L0_ffn_in['bias'], 'L0_ffn_gate_w': _L0_ffn_in['gate_w'], 'L0_ffn_up_w': _L0_ffn_in['up_w'], 'L0_ffn_down_w': _L0_ffn_in['down_w'], 'L0_ffn_sh_gate_w': _L0_ffn_in['sh_gate_w'], 'L0_ffn_sh_up_w': _L0_ffn_in['sh_up_w'], 'L0_ffn_sh_down_w': _L0_ffn_in['sh_down_w']}
    _x0 = _d['L0_attn_hidden_states']
    _d['L0_attn_hidden_states'] = jax.random.normal(jax.random.fold_in(jax.random.key(seed), 1), (8, 512, 128), dtype=_x0.dtype)
    del _x0
    return _d

def reference(L0_attn_hidden_states, L0_attn_W_in, L0_attn_W_xproj, L0_attn_W_dt, L0_attn_b_dt, L0_attn_A_log, L0_attn_D, L0_attn_W_out, L0_attn_K_x, L0_attn_b_x, L0_attn_K_z, L0_attn_b_z, L0_ffn_router_w, L0_ffn_bias, L0_ffn_gate_w, L0_ffn_up_w, L0_ffn_down_w, L0_ffn_sh_gate_w, L0_ffn_sh_up_w, L0_ffn_sh_down_w):

    def _L0_attn_ref(hidden_states, W_in, W_xproj, W_dt, b_dt, A_log, D, W_out, K_x, b_x, K_z, b_z):
        import jax, jax.numpy as jnp
        import numpy as np
        import math
        D_MODEL = 128
        D_STATE = 16
        D_CONV = 4
        EXPAND = 2
        D_INNER = EXPAND * D_MODEL
        D_HALF = D_INNER // 2
        DT_RANK = math.ceil(D_MODEL / 16)
        BATCH = 4
        SEQLEN = 128

        def _dwconv_same(x, K, b):
            k = K.shape[-1]
            y = jax.lax.conv_general_dilated(x, K, window_strides=(1,), padding=[((k - 1) // 2, k // 2)], dimension_numbers=('NCH', 'OIH', 'NCH'), feature_group_count=x.shape[1])
            return y + b[None, :, None]

        def _selective_scan(u, delta, A, Bm, Cm, Dp):
            dA = jnp.exp(jnp.einsum('bdl,dn->lbdn', delta, A))
            dBu = jnp.einsum('bdl,bnl,bdl->lbdn', delta, Bm, u)
            Ct = jnp.transpose(Cm, (2, 0, 1))
            h0 = jnp.zeros(dA.shape[1:], dA.dtype)

            def step(h, inp):
                dA_t, dBu_t, C_t = inp
                h = dA_t * h + dBu_t
                return (h, jnp.einsum('bdn,bn->bd', h, C_t))
            _, ys = jax.lax.scan(step, h0, (dA, dBu, Ct))
            y = jnp.transpose(ys, (1, 2, 0))
            return y + u * Dp[None, :, None]
        xz = jnp.transpose(hidden_states @ W_in, (0, 2, 1))
        x, z = jnp.split(xz, 2, axis=1)
        A = -jnp.exp(A_log)
        x = jax.nn.gelu(_dwconv_same(x, K_x, b_x), approximate=False)
        z = jax.nn.gelu(_dwconv_same(z, K_z, b_z), approximate=False)
        x_dbl = jnp.einsum('bdl,de->ble', x, W_xproj)
        dt, Bm, Cm = jnp.split(x_dbl, [DT_RANK, DT_RANK + D_STATE], axis=-1)
        dt = jnp.transpose(dt @ W_dt, (0, 2, 1))
        Bm = jnp.transpose(Bm, (0, 2, 1))
        Cm = jnp.transpose(Cm, (0, 2, 1))
        delta = jax.nn.softplus(dt + b_dt[None, :, None])
        y = _selective_scan(x, delta, A, Bm, Cm, D)
        y = jnp.transpose(jnp.concatenate([y, z], axis=1), (0, 2, 1))
        return y @ W_out

    def _L0_ffn_ref(hidden_states, router_w, bias, gate_w, up_w, down_w, sh_gate_w, sh_up_w, sh_down_w):
        import jax, jax.numpy as jnp
        import numpy as np
        B, S, D = (1, 256, 128)
        E, F = (16, 128)
        NG, TKG, K = (4, 2, 4)
        NSH = 2
        SCALE = 2.5
        STD = 0.02
        EPG = E // NG

        def _route(x_flat, router_w, bias):
            logits = x_flat.astype(jnp.float32) @ router_w.T
            scores = jax.nn.sigmoid(logits)
            s = scores + bias[None, :]
            sg = s.reshape(-1, NG, EPG)
            group_score = jax.lax.top_k(sg, 2)[0].sum(-1)
            gidx = jax.lax.top_k(group_score, TKG)[1]
            gmask = jnp.sum(jax.nn.one_hot(gidx, NG, dtype=jnp.float32), axis=1) > 0
            emask = jnp.repeat(gmask, EPG, axis=1)
            masked = jnp.where(emask, s, -1.0)
            topk_idx = jax.lax.top_k(masked, K)[1]
            tw = jnp.take_along_axis(scores, topk_idx, axis=1)
            tw = tw / (tw.sum(-1, keepdims=True) + 1e-20)
            tw = tw * SCALE
            return (topk_idx, tw)
        x = hidden_states.reshape(-1, D)
        topk_idx, tw = _route(x, router_w, bias)
        combine = (jax.nn.one_hot(topk_idx, E, dtype=tw.dtype) * tw[..., None]).sum(1)
        h = jnp.einsum('td,edf->etf', x, gate_w)
        u = jnp.einsum('td,edf->etf', x, up_w)
        y = jnp.einsum('etf,efd->etd', jax.nn.silu(h) * u, down_w)
        routed = jnp.einsum('etd,te->td', y, combine)
        sh = jax.nn.silu(x @ sh_gate_w) * (x @ sh_up_w) @ sh_down_w
        return (routed + sh).reshape(hidden_states.shape)
    x = L0_attn_hidden_states
    x = x + 0.5 * _L0_ffn_ref(_layernorm(x, axis=-1), L0_ffn_router_w, L0_ffn_bias, L0_ffn_gate_w, L0_ffn_up_w, L0_ffn_down_w, L0_ffn_sh_gate_w, L0_ffn_sh_up_w, L0_ffn_sh_down_w)
    x = x + _L0_attn_ref(_layernorm(x, axis=-1), L0_attn_W_in, L0_attn_W_xproj, L0_attn_W_dt, L0_attn_b_dt, L0_attn_A_log, L0_attn_D, L0_attn_W_out, L0_attn_K_x, L0_attn_b_x, L0_attn_K_z, L0_attn_b_z)
    x = x + 0.5 * _L0_ffn_ref(_layernorm(x, axis=-1), L0_ffn_router_w, L0_ffn_bias, L0_ffn_gate_w, L0_ffn_up_w, L0_ffn_down_w, L0_ffn_sh_gate_w, L0_ffn_sh_up_w, L0_ffn_sh_down_w)
    return x

_drawn_inputs = setup_inputs


def setup_inputs(seed=0):
    import zlib

    import numpy as np

    out = dict(_drawn_inputs(seed))
    spreads = {'L0_attn_D': (1.0, 0.2),
     'L0_attn_b_x': (0.0, 0.1),
     'L0_attn_b_z': (0.0, 0.1),
     'L0_ffn_bias': (0.0, 0.8)}
    factors = {'L0_attn_W_xproj': 4.737,
     'L0_attn_W_dt': 8.0,
     'L0_attn_b_dt': 8.0,
     'L0_attn_A_log': 8.0,
     'L0_ffn_router_w': 8.0,
     'L0_ffn_gate_w': 8.0,
     'L0_ffn_up_w': 8.0,
     'L0_ffn_down_w': 8.0,
     'L0_ffn_sh_gate_w': 7.472,
     'L0_ffn_sh_up_w': 7.369,
     'L0_ffn_sh_down_w': 7.382}
    for name, (base, spread) in spreads.items():
        noise = np.random.default_rng([zlib.crc32(name.encode()), seed]).standard_normal(out[name].shape)
        drawn = base * np.exp(spread * noise) if base else spread * noise
        out[name] = jnp.asarray(drawn.astype(out[name].dtype))
    for name, factor in factors.items():
        out[name] = (out[name] * factor).astype(out[name].dtype)
    return out
```

```python
import numpy as np
import concourse.bass as bass
from concourse import mybir
from contextlib import ExitStack

FP32 = mybir.dt.float32
F32R = mybir.dt.float32r
BF16 = mybir.dt.bfloat16
ALU = mybir.AluOpType
ACT = mybir.ActivationFunctionType
AX = mybir.AxisListType

P = 128
D = 128
BATCH, SEQ = 8, 512
TT = SEQ // P
E, NSH = 16, 2
NE = E + NSH
GROUPS, TOP_EXPERTS, TOP_GROUPS = 4, 4, 2
EPG = E // GROUPS
ROUTE_SCALE = 2.5
NS, RANK, TAPS = 16, 8, 4
EPS = 1e-5
LAG = 2
PARTS = 3
PAIRS = NS // 2
ARTANH = (2.000000007920744, 0.6666631469061967, 0.4002490989378386, 0.2796060834260729, 0.2817830977129628)
LN_STEPS = 2 * TT + 1


class Steps:

    def __init__(self, eng, sem, base):
        self.eng, self.sem, self.base, self.n = eng, sem, base, 0

    def do(self, ins):
        ins.then_inc(self.sem, 1)
        self.n += 1

    def settle(self):
        self.eng.wait_ge(self.sem, self.base + self.n)

    def settle_apart(self):
        self.settle()
        self.eng.sem_inc(self.sem, 1)
        self.n += 1


def program(nc, x_in, w_in, w_xproj, w_dt, b_dt, a_log, d_skip, w_out, k_x, b_x, k_z, b_z,
            router_w, route_bias, gate_w, up_w, down_w, sh_gate_w, sh_up_w, sh_down_w, out):
    ctx = ExitStack()
    with ctx:
        def sb(name, shape, dt=FP32):
            return ctx.enter_context(nc.sbuf_tensor(name, shape, dt))

        def sem(name):
            return ctx.enter_context(nc.semaphore(name))

        x_sb = sb("x_sb", [P, BATCH + 2, TT, D])
        ident = sb("ident", [P, P])
        ident_bf = sb("ident_bf", [P, P], BF16)
        w_hi = sb("w_hi", [P, NE, 3, P], F32R)
        w_lo = sb("w_lo", [P, NE, 3, P], F32R)
        stage = sb("stage", [P, NE, 3, P])
        xn = sb("xn", [P, TT, D])
        stats = sb("stats", [P, TT, 6])
        mean_var = sb("mean_var", [P, TT, 2])
        var_eps = sb("var_eps", [P, TT])
        rstd = sb("rstd", [P, TT])
        minus_half = sb("minus_half", [P, TT])
        bank = [ctx.enter_context(nc.psum_tensor(f"bank{n}", [P, 2, SEQ], FP32)) for n in range(4)]

        router_sb = sb("router_sb", [P, E])
        bias_sb = sb("bias_sb", [P, TT, E])
        sel_e = sb("sel_e", [P, E, P], BF16)
        before = sb("before", [P, GROUPS, GROUPS])
        same_tile = sb("same_tile", [P, TT, E])
        xt = sb("xt", [P, SEQ])
        x_hi = sb("x_hi", [P, SEQ], F32R)
        x_lo = sb("x_lo", [P, SEQ], F32R)
        sg = sb("sg", [P, 2, SEQ])
        act = sb("act", [P, 2, SEQ])
        act_hi = sb("act_hi", [P, 3, SEQ], F32R)
        act_lo = sb("act_lo", [P, 3, SEQ], F32R)
        out_t = sb("out_t", [P, SEQ])
        c_t = sb("c_t", [P, SEQ], BF16)
        c_parts = sb("c_parts", [P, TT, P], BF16)
        th = sb("th", [P, TT, E])
        score = sb("score", [P, TT, E])
        biased = sb("biased", [P, TT, E])
        pair_sum = sb("pair_sum", [P, TT * GROUPS, 6])
        g_score = sb("g_score", [P, TT, GROUPS])
        g_ge = sb("g_ge", [P, TT, GROUPS, GROUPS])
        g_gt = sb("g_gt", [P, TT, GROUPS, GROUPS])
        g_rank = sb("g_rank", [P, TT * GROUPS])
        g_in = sb("g_in", [P, TT * GROUPS])
        masked = sb("masked", [P, TT, E])
        top8 = sb("top8", [P, TT, 8])
        above = sb("above", [P, TT, E])
        tied = sb("tied", [P, TT, E])
        n_above = sb("n_above", [P, TT])
        tie_at = sb("tie_at", [P, TT, E])
        picked = sb("picked", [P, TT, E])
        total = sb("total", [P, TT])
        comb = sb("comb", [P, TT, E])
        rest = sb("rest", [P, TT, E])

        w_in_sb = sb("w_in_sb", [P, 2, P])
        taps_row = sb("taps_row", [P, 2, P, TAPS])
        w_tap = sb("w_tap", [P, 2, TAPS, P])
        w_xp = sb("w_xp", [P, RANK + 2 * NS])
        w_xp_t = sb("w_xp_t", [RANK, P])
        w_dt_sb = sb("w_dt_sb", [RANK, P])
        w_delta = sb("w_delta", [P, P])
        w_out_sb = sb("w_out_sb", [P, 2, D])
        b_x_sb = sb("b_x_sb", [P, 1])
        b_z_sb = sb("b_z_sb", [P, 1])
        b_dt_sb = sb("b_dt_sb", [P, 1])
        d_sb = sb("d_sb", [P, 1])
        a_exp = sb("a_exp", [P, NS])
        a_neg = sb("a_neg", [P, NS])
        sel_n = sb("sel_n", [P, 2 * NS, P], BF16)
        x_pad = sb("x_pad", [P, SEQ + TAPS - 1])
        u = [sb(f"u{n}", [P, SEQ]) for n in range(2)]
        z = [sb(f"z{n}", [P, SEQ]) for n in range(2)]
        delta = [sb(f"delta{n}", [P, SEQ]) for n in range(2)]
        du = [sb(f"du{n}", [P, SEQ]) for n in range(2)]
        bc_parts = [sb(f"bc_parts{n}", [P, SEQ], BF16) for n in range(2)]
        y_sb = sb("y_sb", [P, SEQ])

        ld_x, ld_xr = sem("ld_x"), sem("ld_xr")
        ld_w = [sem(f"ld_w{q}") for q in range(NE)]
        ld_m, ld_b = sem("ld_m"), sem("ld_b")
        c_pool, c_zero, c_hi, c_lo = sem("c_pool"), sem("c_zero"), sem("c_hi"), sem("c_lo")
        m_pe, m_act, m_dve = sem("m_pe"), sem("m_act"), sem("m_dve")

        SMALL_LOADS = TT + 11

        def load_expert(eng, q):
            if q < NSH:
                cols = slice(q * P, (q + 1) * P)
                srcs = (sh_gate_w[:, cols], sh_up_w[:, cols], sh_down_w[cols, :])
            else:
                srcs = (gate_w[q - NSH], up_w[q - NSH], down_w[q - NSH])
            for n, src in enumerate(srcs):
                eng.dma_start(stage[:, q, n, :], src).then_inc(ld_w[q], 16)

        with nc.Block() as block:
            @block.sync
            def _(sp):
                sp.dma_start(x_sb[:, 1], x_in[0].rearrange("(t p) d -> p t d", p=P)).then_inc(ld_x, 16)
                sp.dma_start(router_sb[:, :], router_w).then_inc(ld_m, 16)
                for q in range(0, NE, 2):
                    load_expert(sp, q)
                for b in range(1, BATCH):
                    sp.dma_start(x_sb[:, b + 1], x_in[b].rearrange("(t p) d -> p t d", p=P)).then_inc(ld_xr, 16)
                sp.wait_ge(ld_xr, 16 * (BATCH - 1))

            @block.scalar
            def _(act_e):
                for q in range(1, NE, 2):
                    load_expert(act_e, q)
                for q in range(NE):
                    act_e.wait_ge(ld_w[q], 48)
                    nc.scalar.activation(w_hi[:, q], stage[:, q], ACT.Copy).then_inc(c_hi, 1)
                act_e.wait_ge(ld_b, 16 * SMALL_LOADS)
                nc.scalar.activation(a_exp[:, :], a_neg[:, :], ACT.Exp).then_inc(m_act, 1)
                act_e.wait_ge(m_pe, 1)
                nc.scalar.activation(w_xp_t[:, :], bank[0][0:RANK, 0, 0:P], ACT.Copy).then_inc(m_act, 1)
                act_e.wait_ge(m_pe, 2)
                nc.scalar.activation(w_delta[:, :], bank[1][:, 0, 0:P], ACT.Copy).then_inc(m_act, 1)

            @block.gpsimd
            def _(pool):
                for t in range(TT):
                    pool.dma_start(bias_sb[:, t, :], route_bias.partition_broadcast(P)).then_inc(ld_b, 16)
                pool.dma_start(w_in_sb[:, :, :], w_in.rearrange("d (h c) -> d h c", h=2)).then_inc(ld_b, 16)
                for h, k in enumerate((k_x, k_z)):
                    pool.dma_start(taps_row[:, h, :, :].rearrange("p c k -> p (c k)"),
                                   k.partition_broadcast(P)).then_inc(ld_b, 16)
                pool.dma_start(w_xp[:, :], w_xproj).then_inc(ld_b, 16)
                pool.dma_start(w_dt_sb[:, :], w_dt).then_inc(ld_b, 16)
                pool.dma_start(w_out_sb[:, :, :], w_out.rearrange("(h c) d -> c h d", h=2)).then_inc(ld_b, 16)
                pool.dma_start(b_x_sb[:, :], b_x).then_inc(ld_b, 16)
                pool.dma_start(b_z_sb[:, :], b_z).then_inc(ld_b, 16)
                pool.dma_start(d_sb[:, :], d_skip).then_inc(ld_b, 16)
                pool.dma_start(a_neg[:, :], a_log).then_inc(ld_b, 16)
                pool.dma_start(b_dt_sb[:, :], b_dt).then_inc(ld_b, 16)
                steps = Steps(pool, c_pool, 0)
                for m in (ident, ident_bf, sel_e, sel_n):
                    steps.do(nc.gpsimd.memset(m[:], 0.0))
                steps.do(nc.gpsimd.memset(before[:], 1.0))
                steps.do(nc.gpsimd.memset(minus_half[:], -0.5))
                steps.settle()
                for m in (ident, ident_bf):
                    steps.do(nc.gpsimd.affine_select(out=m[:], in_=m[:], compare_op=ALU.not_equal, fill=1.0,
                                                     base=0, pattern=[[-1, P]], channel_multiplier=1))
                steps.do(nc.gpsimd.affine_select(out=before[:], in_=before[:], compare_op=ALU.is_gt, fill=0.0,
                                                 base=0, pattern=[[1, GROUPS], [-1, GROUPS]],
                                                 channel_multiplier=0))
                for part in range(PARTS):
                    steps.do(nc.gpsimd.affine_select(out=sel_e[:], in_=sel_e[:], compare_op=ALU.not_equal,
                                                     fill=1.0, base=-part * E, pattern=[[-1, E], [0, P]],
                                                     channel_multiplier=1))
                    steps.do(nc.gpsimd.affine_select(out=sel_n[:], in_=sel_n[:], compare_op=ALU.not_equal,
                                                     fill=1.0, base=-part * 2 * NS,
                                                     pattern=[[-1, 2 * NS], [0, P]], channel_multiplier=1))
                    steps.settle()

            @block.vector
            def _(dve):
                zero = Steps(dve, c_zero, 0)
                for m in (x_sb[:, 0], x_sb[:, BATCH + 1], c_parts[:], act_hi[:, 1:3].bitcast(FP32),
                          act_lo[:, 1:3].bitcast(FP32), x_pad[:, 0:1], x_pad[:, SEQ + 1:SEQ + TAPS - 1],
                          bc_parts[0][:], bc_parts[1][:], u[1][:], z[1][:], y_sb[:]):
                    zero.do(nc.vector.memset(m, 0.0))
                zero.do(nc.vector.memset(same_tile[:], 1.0))
                zero.settle()
                zero.do(nc.vector.memset(same_tile[:, :, 0:1], 0.0))
                for q in range(NE):
                    dve.wait_ge(c_hi, q + 1)
                    nc.vector.tensor_tensor(w_lo[:, q], stage[:, q], w_hi[:, q].bitcast(FP32),
                                            ALU.subtract).then_inc(c_lo, 1)
                dve.wait_ge(ld_b, 16 * SMALL_LOADS)
                for h in range(2):
                    for k in range(TAPS):
                        nc.vector.tensor_tensor(w_tap[:, h, k, :], w_in_sb[:, h, :], taps_row[:, h, :, k],
                                                ALU.mult).then_inc(m_dve, 1)
                dve.wait_ge(m_act, 1)
                nc.vector.tensor_scalar(a_neg[:, :], a_exp[:, :], -1.0, None, ALU.mult).then_inc(m_dve, 1)

            @block.tensor
            def _(pe):
                pe.wait_ge(c_pool, 8)
                pe.wait_ge(ld_b, 16 * SMALL_LOADS)
                nc.tensor.transpose(bank[0][0:RANK, 0, 0:P], w_xp[:, 0:RANK], ident[:, :]).then_inc(m_pe, 1)
                pe.wait_ge(m_act, 2)
                nc.tensor.matmul(bank[1][:, 0, 0:P], w_xp_t[:, :], w_dt_sb[:, :], start=True,
                                 stop=True).then_inc(m_pe, 1)

        moe = dict(locals())
        moe_phase(nc, ctx, "f1", moe, None)
        mamba_phase(nc, ctx, moe)
        moe_phase(nc, ctx, "f2", moe, out)


def norm_stats(nc, steps, x_sb, slot, stats, mean_var, var_eps, ready):
    for t in range(TT):
        steps.do(nc.vector.bn_stats(stats[:, t, :], x_sb[:, slot, t, :]))
    steps.settle_apart()
    for t in range(TT):
        steps.do(nc.vector.bn_aggr(mean_var[:, t, :], stats[:, t, :]))
    steps.settle()
    nc.vector.tensor_scalar(var_eps[:, :], mean_var[:, :, 1], EPS, None, ALU.add).then_inc(ready, 1)


def norm_apply(nc, x_sb, slot, xn, mean_var, rstd, done):
    for t in range(TT):
        nc.vector.tensor_scalar(xn[:, t, :], x_sb[:, slot, t, :], mean_var[:, t, 0:1], rstd[:, t:t + 1],
                                ALU.subtract, ALU.mult).then_inc(done, 1)


def moe_phase(nc, ctx, tag, m, out):
    (x_sb, ident, ident_bf, w_hi, w_lo, xn, stats, mean_var, var_eps, rstd, minus_half, bank, router_sb,
     bias_sb, sel_e, before, same_tile, xt, x_hi, x_lo, sg, act, act_hi, act_lo, out_t, c_t, c_parts, th,
     score, biased, pair_sum, g_score, g_ge, g_gt, g_rank, g_in, masked, top8, above, tied, n_above, tie_at,
     picked, total, comb, rest) = (m[n] for n in (
         "x_sb ident ident_bf w_hi w_lo xn stats mean_var var_eps rstd minus_half bank router_sb bias_sb "
         "sel_e before same_tile xt x_hi x_lo sg act act_hi act_lo out_t c_t c_parts th score biased "
         "pair_sum g_score g_ge g_gt g_rank g_in masked top8 above tied n_above tie_at picked total comb "
         "rest").split())
    h_bank, u_bank, c_bank = (bank[n] for n in range(3))
    acc, misc = bank[3][:, 0, :], bank[3][:, 1, :]
    misc_bf = misc.bitcast(BF16)

    def sem(name):
        return ctx.enter_context(nc.semaphore(f"{tag}_{name}"))

    h_ready, u_ready, cb_ready = sem("h_ready"), sem("u_ready"), sem("cb_ready")
    sg_ready = sem("sg_ready")
    w_done = sem("w_done")
    act_ready = sem("act_ready")
    hi_ready = sem("hi_ready")
    lo_ready = sem("lo_ready")
    down_done = sem("down_done")
    acc_read, ot_ready, x_added = sem("acc_read"), sem("ot_ready"), sem("x_added")
    var_ready, rstd_ready, xn_ready = sem("var_ready"), sem("rstd_ready"), sem("xn_ready")
    xt_ready, xt_copied, logits_ready, tanh_ready = (
        sem("xt_ready"), sem("xt_copied"), sem("logits_ready"), sem("tanh_ready"))
    parts_ready, ct_ready, ct_copied, x_split = (
        sem("parts_ready"), sem("ct_ready"), sem("ct_copied"), sem("x_split"))
    norm_step, route_step, stored = sem("norm_step"), sem("route_step"), sem("stored")
    ROUTE_STEPS = 34

    with nc.Block() as block:
        @block.sync
        def _(sp):
            if out is not None:
                rows = out.rearrange("b (t p) d -> b p t d", p=P)
                with sp.Fori(0, BATCH) as i:
                    sp.wait_ge(x_added, i + 2)
                    sp.dma_start(rows[i], x_sb[:, i + 1]).then_inc(stored, 16)
                sp.wait_ge(stored, 16 * BATCH)

        @block.gpsimd
        def _(pool):
            def norm_root(r):
                pool.wait_ge(var_ready, r + 1)
                nc.gpsimd.tensor_tensor(rstd[:, :], var_eps[:, :], minus_half[:, :], ALU.pow).then_inc(rstd_ready, 1)

            norm_root(0)
            with pool.Fori(0, BATCH) as i:
                for k in range(NE):
                    if k == 4:
                        norm_root(i + 1)
                    g = i * NE + k
                    pool.wait_ge(hi_ready, g + 1)
                    nc.gpsimd.tensor_tensor(act_lo[:, k % 3], act[:, k % 2], act_hi[:, k % 3].bitcast(FP32),
                                            ALU.subtract).then_inc(lo_ready, 1)

        @block.scalar
        def _(ae):
            nc.scalar.preload_act_table_set("silu_and_others")

            def copy_xt(r):
                ae.wait_ge(xt_ready, r + 1)
                nc.scalar.activation(xt[:, :], misc, ACT.Copy).then_inc(xt_copied, 1)

            def tanh(r):
                ae.wait_ge(logits_ready, r + 1)
                nc.scalar.activation(th[:].rearrange("p t e -> p (t e)"), misc[:, 0:TT * E], ACT.Tanh,
                                     scale=0.5).then_inc(tanh_ready, 1)

            def read_acc(i):
                nc.scalar.activation(out_t[:, :], acc, ACT.Copy, scale=0.5).then_inc(acc_read, 1)

            copy_xt(0)
            tanh(0)
            with ae.Fori(0, BATCH) as i:
                for k in range(NE):
                    g = i * NE + k
                    if k == 0:
                        ae.wait_ge(ct_ready, i + 1)
                        nc.scalar.activation(c_t[:, :], misc_bf[:, 0:SEQ], ACT.Copy).then_inc(ct_copied, 1)
                    ae.wait_ge(h_ready, g + 1)
                    ae.wait_ge(act_ready, g + 1)
                    nc.scalar.activation(sg[:, k % 2], h_bank[:, k % 2], ACT.Silu).then_inc(sg_ready, 1)
                    for j in ([k - 1] if k else []) + ([k] if k == NE - 1 else []):
                        ae.wait_ge(act_ready, i * NE + j + 3)
                        ae.wait_ge(down_done, i * NE + j + 1)
                        nc.scalar.activation(act_hi[:, j % 3], act[:, j % 2], ACT.Copy).then_inc(hi_ready, 1)
                    if k == 2:
                        ae.wait_ge(down_done, i * NE + 3)
                        read_acc(i)
                    if k == 7:
                        ae.wait_ge(x_split, 2 * i + 2)
                        copy_xt(i + 1)
                    if k == 8:
                        tanh(i + 1)
            ae.wait_ge(down_done, BATCH * NE + 3)
            ae.wait_ge(ot_ready, BATCH)
            read_acc(BATCH)

        @block.vector
        def _(dve):
            dve.sem_inc(sg_ready, 2)
            dve.sem_inc(w_done, 2)
            dve.sem_inc(act_ready, 2)
            dve.sem_inc(lo_ready, 2)
            dve.sem_inc(down_done, 1)

            def stats_of(r, slot):
                steps = Steps(dve, norm_step, r * LN_STEPS)
                norm_stats(nc, steps, x_sb, slot, stats, mean_var, var_eps, var_ready)

            def apply_to(r, slot):
                dve.wait_ge(rstd_ready, r + 1)
                norm_apply(nc, x_sb, slot, xn, mean_var, rstd, xn_ready)

            def route(r, first=False):
                s = Steps(dve, route_step, r * ROUTE_STEPS)
                flat = lambda a: a[:].rearrange("p t e -> p (t e)")
                grouped = lambda a: a[:].rearrange("p t (g e) -> p (t g) e", g=GROUPS)
                gs = g_score[:].rearrange("p t g -> p (t g)")
                dve.wait_ge(tanh_ready, r + 1)
                s.do(nc.vector.tensor_scalar(flat(score), flat(th), 0.5, 0.5, ALU.mult, ALU.add))
                s.settle()
                s.do(nc.vector.tensor_tensor(flat(biased), flat(score), flat(bias_sb), ALU.add))
                s.settle()
                b4, at = grouped(biased), 0
                for gap in range(1, EPG):
                    n = EPG - gap
                    s.do(nc.vector.tensor_tensor(pair_sum[:, :, at:at + n], b4[:, :, 0:n], b4[:, :, gap:EPG],
                                                 ALU.add))
                    at += n
                s.settle()
                s.do(nc.vector.tensor_reduce(gs, pair_sum[:], AX.X, ALU.max))
                s.settle()
                yield
                other = g_score[:].unsqueeze(2).broadcast_to([P, TT, GROUPS, GROUPS])
                own = g_score[:].unsqueeze(3).broadcast_to([P, TT, GROUPS, GROUPS])
                s.do(nc.vector.tensor_tensor(g_ge[:], other, own, ALU.is_ge))
                s.do(nc.vector.tensor_tensor(g_gt[:], other, own, ALU.is_gt))
                s.settle()
                s.do(nc.vector.tensor_tensor(g_ge[:], g_ge[:],
                                             before[:].unsqueeze(1).broadcast_to([P, TT, GROUPS, GROUPS]),
                                             ALU.mult))
                s.settle()
                s.do(nc.vector.tensor_tensor(g_ge[:], g_ge[:], g_gt[:], ALU.max))
                s.settle()
                s.do(nc.vector.tensor_reduce(g_rank[:], g_ge[:].rearrange("p t g h -> p (t g) h"), AX.X, ALU.add))
                s.settle()
                yield
                s.do(nc.vector.tensor_scalar(g_in[:], g_rank[:], float(TOP_GROUPS), None, ALU.is_lt))
                s.settle()
                g_in_e = g_in[:].unsqueeze(2).broadcast_to([P, TT * GROUPS, EPG])
                s.do(nc.vector.tensor_tensor(grouped(masked), grouped(biased), g_in_e, ALU.mult))
                s.settle()
                s.do(nc.vector.scalar_tensor_tensor(grouped(masked), g_in_e, -1.0, grouped(masked),
                                                    ALU.add, ALU.add))
                s.settle_apart()
                for t in range(TT):
                    s.do(nc.vector.max(top8[:, t, :], masked[:, t, :]))
                s.settle()
                yield
                fourth = top8[:, :, TOP_EXPERTS - 1:TOP_EXPERTS].broadcast_to([P, TT, E])
                s.do(nc.vector.tensor_tensor(above[:], masked[:], fourth, ALU.is_gt))
                s.do(nc.vector.tensor_tensor(tied[:], masked[:], fourth, ALU.is_equal))
                s.settle()
                s.do(nc.vector.tensor_reduce(n_above[:], above[:], AX.X, ALU.add))
                s.do(nc.vector.tensor_tensor_scan(flat(tie_at), flat(same_tile), flat(tied), 0.0,
                                                  ALU.mult, ALU.add))
                s.settle()
                s.do(nc.vector.tensor_tensor(tie_at[:], tie_at[:],
                                             n_above[:].unsqueeze(2).broadcast_to([P, TT, E]), ALU.add))
                s.settle()
                s.do(nc.vector.scalar_tensor_tensor(flat(picked), flat(tie_at), float(TOP_EXPERTS), flat(tied),
                                                    ALU.is_le, ALU.mult))
                s.settle()
                yield
                s.do(nc.vector.tensor_tensor(picked[:], picked[:], above[:], ALU.add))
                s.settle()
                s.do(nc.vector.tensor_tensor(picked[:], picked[:], score[:], ALU.mult))
                s.settle()
                s.do(nc.vector.tensor_reduce(total[:], picked[:], AX.X, ALU.add))
                s.settle()
                s.do(nc.vector.tensor_scalar(total[:], total[:], 1e-20, None, ALU.add))
                s.settle()
                s.do(nc.vector.reciprocal(total[:], total[:]))
                s.settle()
                s.do(nc.vector.scalar_tensor_tensor(comb[:], picked[:], ROUTE_SCALE,
                                                    total[:].unsqueeze(2).broadcast_to([P, TT, E]),
                                                    ALU.mult, ALU.mult))
                s.settle()
                yield
                if not first:
                    dve.wait_ge(ct_ready, r)
                s.do(nc.vector.tensor_copy(c_parts[:, :, 0:E], comb[:]))
                s.settle()
                s.do(nc.vector.tensor_tensor(rest[:], comb[:], c_parts[:, :, 0:E], ALU.subtract))
                s.settle()
                s.do(nc.vector.tensor_copy(c_parts[:, :, E:2 * E], rest[:]))
                s.settle()
                nc.vector.tensor_tensor(c_parts[:, :, 2 * E:3 * E], rest[:], c_parts[:, :, E:2 * E],
                                        ALU.subtract).then_inc(parts_ready, 1)
                assert s.n == ROUTE_STEPS, s.n
                yield

            def split_x(r):
                dve.wait_ge(xt_copied, r + 1)
                nc.vector.tensor_copy(x_hi[:, :], xt[:, :]).then_inc(x_split, 1)
                dve.wait_ge(x_split, 2 * r + 1)
                nc.vector.tensor_tensor(x_lo[:, :], xt[:, :], x_hi[:, :].bitcast(FP32),
                                        ALU.subtract).then_inc(x_split, 1)

            def add_rows(i):
                dve.wait_ge(ot_ready, i + 1)
                nc.vector.tensor_tensor(x_sb[:, i], x_sb[:, i], misc.rearrange("p (t d) -> p t d", t=TT),
                                        ALU.add).then_inc(x_added, 1)

            stats_of(0, 1)
            apply_to(0, 1)
            for _ in route(0, first=True):
                pass
            split_x(0)
            with dve.Fori(0, BATCH) as i:
                routing = route(i + 1)
                for k in range(NE):
                    g = i * NE + k
                    dve.wait_ge(sg_ready, g + 3)
                    if k >= NSH:
                        r = i * E + (k - NSH)
                        dve.wait_ge(cb_ready, r + 1)
                        nc.vector.tensor_tensor(sg[:, k % 2], sg[:, k % 2], c_bank[:, k % 2],
                                                ALU.mult).then_inc(w_done, 1)
                    dve.wait_ge(u_ready, g + 1)
                    if k == NE - 1:
                        split_x(i + 1)
                    if k >= NSH:
                        dve.wait_ge(w_done, r + 3)
                    dve.wait_ge(lo_ready, g + 1)
                    nc.vector.tensor_tensor(act[:, k % 2], sg[:, k % 2], u_bank[:, k % 2],
                                            ALU.mult).then_inc(act_ready, 1)
                    if k == 3:
                        stats_of(i + 1, i + 2)
                    if k == 4:
                        add_rows(i)
                    if k == 5:
                        dve.wait_ge(xt_ready, i + 1)
                        apply_to(i + 1, i + 2)
                    if 9 <= k <= 14:
                        next(routing)
            add_rows(BATCH)
            dve.wait_ge(x_added, BATCH + 1)

        @block.tensor
        def _(pe):
            def transpose_xn(r):
                pe.wait_ge(xn_ready, TT * (r + 1))
                for t in range(TT):
                    last = nc.tensor.transpose(misc[:, t * P:(t + 1) * P], xn[:, t, :], ident[:, :])
                last.then_inc(xt_ready, 1)

            def logits(r):
                pe.wait_ge(xt_copied, r + 1)
                for t in range(TT):
                    last = nc.tensor.matmul(misc[:, t * E:(t + 1) * E], xt[:, t * P:(t + 1) * P],
                                            router_sb[:, :], start=True, stop=True)
                last.then_inc(logits_ready, 1)

            def transpose_parts(r):
                pe.wait_ge(tanh_ready, r + 1)
                pe.wait_ge(parts_ready, r + 1)
                for t in range(TT):
                    last = nc.tensor.transpose(misc_bf[:, t * P:(t + 1) * P], c_parts[:, t, :], ident_bf[:, :])
                last.then_inc(ct_ready, 1)

            def down(i, k):
                j = k % NE
                pe.wait_ge(lo_ready, i * NE + k + 3)
                if k == 0:
                    pe.wait_ge(acc_read, i + 1)
                dt = w_hi[:, j, 2, :], w_lo[:, j, 2, :]
                first, last = j == 0, j == NE - 1
                nc.tensor.matmul(acc, dt[0], act_hi[:, j % 3], start=first, stop=False, skip_group_check=True)
                nc.tensor.matmul(acc, dt[1], act_hi[:, j % 3], start=False, stop=False, skip_group_check=True)
                nc.tensor.matmul(acc, dt[0], act_lo[:, j % 3], start=False, stop=last,
                                 skip_group_check=True).then_inc(down_done, 1)

            def transpose_out(i):
                pe.wait_ge(acc_read, i + 1)
                for t in range(TT):
                    last = nc.tensor.transpose(misc[:, t * P:(t + 1) * P], out_t[:, t * P:(t + 1) * P], ident[:, :])
                last.then_inc(ot_ready, 1)

            def product(dst, n, k):
                nc.tensor.matmul(dst, w_hi[:, k, n, :], x_hi[:, :], start=True, stop=False)
                nc.tensor.matmul(dst, w_lo[:, k, n, :], x_hi[:, :], start=False, stop=False)
                return nc.tensor.matmul(dst, w_hi[:, k, n, :], x_lo[:, :], start=False, stop=True)

            transpose_xn(0)
            logits(0)
            nc.tensor.matmul(acc, w_hi[:, 0, 2, :], act_hi[:, 1], start=True, stop=True)
            transpose_parts(0)
            with pe.Fori(0, BATCH) as i:
                for k in range(NE):
                    g = i * NE + k
                    if k < LAG:
                        down(i, k - LAG)
                    if k == 0:
                        pe.wait_ge(x_split, 2 * i + 2)
                    pe.wait_ge(sg_ready, g + 1)
                    product(h_bank[:, k % 2], 0, k).then_inc(h_ready, 1)
                    pe.wait_ge(act_ready, g + 1)
                    product(u_bank[:, k % 2], 1, k).then_inc(u_ready, 1)
                    if k >= NSH:
                        r = i * E + (k - NSH)
                        pe.wait_ge(ct_copied, i + 1)
                        pe.wait_ge(w_done, r + 1)
                        nc.tensor.matmul(c_bank[:, k % 2], sel_e[:, k - NSH, :], c_t[:, :], start=True,
                                         stop=True).then_inc(cb_ready, 1)
                    if k >= LAG:
                        down(i, k - LAG)
                    if k == 3:
                        pe.wait_ge(ct_copied, i + 1)
                        transpose_out(i)
                    if k == 6:
                        pe.wait_ge(x_added, i + 1)
                        transpose_xn(i + 1)
                    if k == 8:
                        logits(i + 1)
                    if k == NE - 1:
                        transpose_parts(i + 1)
            pe.wait_ge(ct_ready, BATCH + 1)
            for k in range(-LAG, 0):
                down(BATCH, k)
            transpose_out(BATCH)


def mamba_phase(nc, ctx, m):
    (x_sb, ident, xn, stats, mean_var, var_eps, rstd, minus_half, bank, w_tap, w_xp, w_delta, w_out_sb,
     b_x_sb, b_z_sb, b_dt_sb, d_sb, a_neg, sel_n, x_pad, u, z, delta, du, bc_parts, y_sb, stage) = (
        m[n] for n in (
            "x_sb ident xn stats mean_var var_eps rstd minus_half bank w_tap w_xp w_delta w_out_sb b_x_sb "
            "b_z_sb b_dt_sb d_sb a_neg sel_n x_pad u z delta du bc_parts y_sb stage").split())
    b_bank, c_bank = bank[0], bank[1]
    y_acc, misc = bank[2][:, 0, :], bank[2][:, 1, :]
    front = bank[3]

    room = stage[:].rearrange("p a b c -> p (a b c)")
    at = [0]

    def place(*shape):
        n = int(np.prod(shape))
        at[0] += n
        v = room[:, at[0] - n:at[0]]
        return v.rearrange("p (a s l) -> p a s l", a=shape[0], s=shape[1]) if len(shape) == 3 else (
            v.rearrange("p (s l) -> p s l", s=shape[0]) if len(shape) == 2 else v)

    decay = place(2, 2, SEQ)
    state_in = place(2, SEQ)
    state = place(2, SEQ)
    state_c = place(2, 2, SEQ)
    soft_abs, soft_relu, soft_e, soft_t = m["sg"][:, 0], m["sg"][:, 1], m["act"][:, 0], m["act"][:, 1]
    soft_q, rest, second = m["out_t"][:, :], m["xt"][:, :], m["c_t"][:, :]
    assert at[0] <= NE * 3 * P

    def sem(name):
        return ctx.enter_context(nc.semaphore(f"mb_{name}"))

    var_ready, rstd_ready, xn_ready, norm_step = (
        sem("var_ready"), sem("rstd_ready"), sem("xn_ready"), sem("norm_step"))
    xt_ready, xt_copied, conv_ready, gated = sem("xt_ready"), sem("xt_copied"), sem("conv_ready"), sem("gated")
    bc_ready, dt_ready = sem("bc_ready"), sem("dt_ready")
    first_part, rest_ready, second_part, parts_ready = (
        sem("first_part"), sem("rest_ready"), sem("second_part"), sem("parts_ready"))
    soft_act, soft_dve, du_ready = sem("soft_act"), sem("soft_dve"), sem("du_ready")
    b_ready, c_ready, decay_ready = sem("b_ready"), sem("c_ready"), sem("decay_ready")
    in_done = sem("in_done")
    scan_done = sem("scan_done")
    mul_done = sem("mul_done")
    sum_done = sem("sum_done")
    out_ready = sem("out_ready")
    y_ready, x_added, zeroed = sem("y_ready"), sem("x_added"), sem("zeroed")
    ACT_SOFT, DVE_SOFT = 3, 10

    with nc.Block() as block:
        @block.gpsimd
        def _(pool):
            with pool.Fori(0, BATCH + 1) as r:
                pool.wait_ge(var_ready, r + 1)
                nc.gpsimd.tensor_tensor(rstd[:, :], var_eps[:, :], minus_half[:, :], ALU.pow).then_inc(rstd_ready, 1)

        @block.scalar
        def _(ae):
            def copy_xt(r):
                ae.wait_ge(xt_ready, r + 1)
                nc.scalar.activation(x_pad[:, 1:SEQ + 1], misc, ACT.Copy).then_inc(xt_copied, 1)

            def gelus(r, q):
                ae.wait_ge(conv_ready, 2 * r + 1)
                nc.scalar.activation(u[q][:, :], front[:, 0, :], ACT.Gelu, bias=b_x_sb[:, 0:1]).then_inc(gated, 1)
                ae.wait_ge(conv_ready, 2 * r + 2)
                nc.scalar.activation(z[q][:, :], front[:, 1, :], ACT.Gelu, bias=b_z_sb[:, 0:1]).then_inc(gated, 1)
                nc.scalar.preload_act_table_set("exp_and_others")

            def parts(r, q):
                ae.wait_ge(bc_ready, r + 1)
                nc.scalar.activation(bc_parts[q][0:2 * NS, :], front[0:2 * NS, 0, :], ACT.Copy).then_inc(first_part, 1)
                ae.wait_ge(rest_ready, r + 1)
                nc.scalar.activation(second[0:2 * NS, :], rest[0:2 * NS, :], ACT.Copy).then_inc(second_part, 1)
                nc.scalar.activation(bc_parts[q][2 * NS:4 * NS, :], rest[0:2 * NS, :], ACT.Copy).then_inc(parts_ready, 1)

            def soft(r):
                base = r * ACT_SOFT
                ae.wait_ge(dt_ready, r + 1)
                nc.scalar.activation(soft_abs, front[:, 1, :], ACT.Abs, bias=b_dt_sb[:, 0:1]).then_inc(soft_act, 1)
                nc.scalar.activation(soft_relu, front[:, 1, :], ACT.Relu, bias=b_dt_sb[:, 0:1]).then_inc(soft_act, 1)
                ae.wait_ge(soft_act, base + 2)
                nc.scalar.activation(soft_e, soft_abs, ACT.Exp, scale=-1.0).then_inc(soft_act, 1)

            def decays(i, n, q):
                ae.wait_ge(scan_done, i * PAIRS + n + 1)
                if n == 0:
                    ae.wait_ge(soft_dve, (i + 1) * DVE_SOFT)
                for s in range(2):
                    nc.scalar.activation(decay[:, n % 2, s, 1:SEQ], delta[q][:, 1:SEQ], ACT.Exp,
                                         scale=a_neg[:, 2 * n + s:2 * n + s + 1]).then_inc(decay_ready, 1)

            copy_xt(0)
            gelus(0, 0)
            parts(0, 0)
            soft(0)
            ae.wait_ge(zeroed, 3)
            with ae.Fori(0, BATCH // 2) as turn:
                for q in range(2):
                    i = turn * 2 + q
                    for n in range(PAIRS):
                        decays(i, n, q)
                        if n == 3:
                            ae.wait_ge(conv_ready, 2 * i + 2)
                            copy_xt(i + 1)
                        if n == 4:
                            ae.wait_ge(y_ready, i + 1)
                            ae.wait_ge(out_ready, i + 2)
                            gelus(i + 1, 1 - q)
                        if n == 5:
                            parts(i + 1, 1 - q)
                            ae.wait_ge(soft_dve, (i + 1) * DVE_SOFT)
                            soft(i + 1)

        @block.vector
        def _(dve):
            def stats_of(r, slot):
                steps = Steps(dve, norm_step, r * LN_STEPS)
                norm_stats(nc, steps, x_sb, slot, stats, mean_var, var_eps, var_ready)

            def apply_to(r, slot):
                dve.wait_ge(rstd_ready, r + 1)
                norm_apply(nc, x_sb, slot, xn, mean_var, rstd, xn_ready)

            def parts(r, q):
                dve.wait_ge(first_part, r + 1)
                nc.vector.tensor_tensor(rest[0:2 * NS, :], front[0:2 * NS, 0, :], bc_parts[q][0:2 * NS, :],
                                        ALU.subtract).then_inc(rest_ready, 1)
                dve.wait_ge(second_part, r + 1)
                nc.vector.tensor_tensor(bc_parts[q][4 * NS:6 * NS, :], rest[0:2 * NS, :], second[0:2 * NS, :],
                                        ALU.subtract).then_inc(parts_ready, 1)

            def soft(r, q):
                count = Steps(dve, soft_dve, r * DVE_SOFT)

                def step(ins):
                    count.do(ins)
                    count.settle()

                dve.wait_ge(soft_act, (r + 1) * ACT_SOFT)
                step(nc.vector.tensor_scalar(soft_t, soft_e, 2.0, None, ALU.add))
                step(nc.vector.reciprocal(soft_t, soft_t))
                step(nc.vector.tensor_tensor(soft_e, soft_e, soft_t, ALU.mult))
                step(nc.vector.tensor_tensor(soft_t, soft_e, soft_e, ALU.mult))
                step(nc.vector.tensor_scalar(soft_q, soft_t, ARTANH[4], ARTANH[3], ALU.mult, ALU.add))
                step(nc.vector.tensor_tensor(soft_q, soft_q, soft_t, ALU.mult))
                for c in (2, 1):
                    step(nc.vector.scalar_tensor_tensor(soft_q, soft_q, ARTANH[c], soft_t, ALU.add, ALU.mult))
                step(nc.vector.scalar_tensor_tensor(soft_q, soft_q, ARTANH[0], soft_e, ALU.add, ALU.mult))
                step(nc.vector.tensor_tensor(delta[q][:, :], soft_q, soft_relu, ALU.add))
                assert count.n == DVE_SOFT
                nc.vector.tensor_tensor(du[q][:, :], delta[q][:, :], u[q][:, :], ALU.mult).then_inc(du_ready, 1)

            dve.sem_inc(scan_done, 2)
            for credited in (mul_done, sum_done, out_ready):
                dve.sem_inc(credited, 1)
            for v in (decay[:, 0, :, 0:1], decay[:, 1, :, 0:1], y_acc):
                nc.vector.memset(v, 0.0).then_inc(zeroed, 1)
            stats_of(0, 1)
            apply_to(0, 1)
            parts(0, 0)
            soft(0, 0)
            with dve.Fori(0, BATCH // 2) as turn:
                for q in range(2):
                    i = turn * 2 + q
                    for n in range(PAIRS):
                        g = i * PAIRS + n
                        dve.wait_ge(b_ready, g + 1)
                        if n == 0:
                            dve.wait_ge(du_ready, i + 1)
                        dve.wait_ge(scan_done, g + 2)
                        nc.vector.tensor_tensor(state_in, du[q][:, :].unsqueeze(1).broadcast_to([P, 2, SEQ]),
                                                b_bank[:], ALU.mult).then_inc(in_done, 1)
                        dve.wait_ge(decay_ready, 2 * g + 2)
                        dve.wait_ge(in_done, g + 1)
                        dve.wait_ge(mul_done, g + 1)
                        nc.vector.tensor_tensor_scan(
                            state.rearrange("p s l -> p (s l)"), decay[:, n % 2].rearrange("p s l -> p (s l)"),
                            state_in.rearrange("p s l -> p (s l)"), 0.0, ALU.mult, ALU.add).then_inc(scan_done, 1)
                        dve.wait_ge(c_ready, g + 1)
                        dve.wait_ge(scan_done, g + 3)
                        if n >= 2:
                            dve.wait_ge(sum_done, g)
                        nc.vector.tensor_tensor(state_c[:, n % 2], state, c_bank[:], ALU.mult).then_inc(mul_done, 1)
                        if n == 0:
                            dve.wait_ge(sum_done, i * PAIRS + 1)
                            dve.wait_ge(out_ready, i + 1)
                            nc.vector.scalar_tensor_tensor(y_sb[:, :], u[1 - q][:, :], d_sb[:, 0:1], y_acc,
                                                           ALU.mult, ALU.add).then_inc(y_ready, 1)
                            stats_of(i + 1, i + 2)
                        if n == 1:
                            dve.wait_ge(xt_ready, i + 1)
                            apply_to(i + 1, i + 2)
                        if n == 2:
                            dve.wait_ge(out_ready, i + 2)
                            nc.vector.tensor_tensor(x_sb[:, i], x_sb[:, i],
                                                    misc.rearrange("p (t d) -> p t d", t=TT),
                                                    ALU.add).then_inc(x_added, 1)
                        if n == 5:
                            parts(i + 1, 1 - q)
                        if n == 6:
                            soft(i + 1, 1 - q)
            dve.wait_ge(sum_done, BATCH * PAIRS + 1)
            dve.wait_ge(out_ready, BATCH + 1)
            nc.vector.scalar_tensor_tensor(y_sb[:, :], u[1][:, :], d_sb[:, 0:1], y_acc, ALU.mult,
                                           ALU.add).then_inc(y_ready, 1)
            dve.wait_ge(out_ready, BATCH + 2)
            nc.vector.tensor_tensor(x_sb[:, BATCH], x_sb[:, BATCH], misc.rearrange("p (t d) -> p t d", t=TT),
                                    ALU.add).then_inc(x_added, 1)
            dve.wait_ge(x_added, BATCH + 1)

        @block.tensor
        def _(pe):
            def transpose_xn(r):
                pe.wait_ge(xn_ready, TT * (r + 1))
                for t in range(TT):
                    last = nc.tensor.transpose(misc[:, t * P:(t + 1) * P], xn[:, t, :], ident[:, :])
                last.then_inc(xt_ready, 1)

            def conv(r):
                pe.wait_ge(xt_copied, r + 1)
                for h in range(2):
                    for k in range(TAPS):
                        last = nc.tensor.matmul(front[:, h, :], w_tap[:, h, k, :], x_pad[:, k:k + SEQ],
                                                start=(k == 0), stop=(k == TAPS - 1))
                    last.then_inc(conv_ready, 1)

            def project(r, q):
                pe.wait_ge(gated, 2 * r + 2)
                nc.tensor.matmul(front[0:2 * NS, 0, :], w_xp[:, RANK:], u[q][:, :], start=True,
                                 stop=True).then_inc(bc_ready, 1)
                nc.tensor.matmul(front[:, 1, :], w_delta[:, :], u[q][:, :], start=True,
                                 stop=True).then_inc(dt_ready, 1)

            def spread(dst, i, n, q, c):
                for s in range(2):
                    last = nc.tensor.matmul(dst[:, s, :], sel_n[:, c * NS + 2 * n + s, :], bc_parts[q][:, :],
                                            start=True, stop=True)
                return last

            def add_states(i, n):
                pe.wait_ge(mul_done, i * PAIRS + n + 2)
                if n == 0:
                    pe.wait_ge(y_ready, i + 1)
                for s in range(2):
                    last = nc.tensor.matmul(y_acc, ident[:, :], state_c[:, n % 2, s, :],
                                            start=(n == 0 and s == 0), stop=(n == PAIRS - 1 and s == 1))
                last.then_inc(sum_done, 1)

            def project_out(i, q):
                pe.wait_ge(y_ready, i + 1)
                for t in range(TT):
                    cols = slice(t * P, (t + 1) * P)
                    nc.tensor.matmul(misc[:, cols], y_sb[:, cols], w_out_sb[:, 0, :], start=True, stop=False)
                    last = nc.tensor.matmul(misc[:, cols], z[1 - q][:, cols], w_out_sb[:, 1, :], start=False,
                                            stop=True)
                last.then_inc(out_ready, 1)

            transpose_xn(0)
            conv(0)
            project(0, 0)
            pe.wait_ge(parts_ready, 2)
            spread(b_bank, 0, 0, 0, 0).then_inc(b_ready, 1)
            pe.wait_ge(zeroed, 3)
            with pe.Fori(0, BATCH // 2) as turn:
                for q in range(2):
                    i = turn * 2 + q
                    for n in range(PAIRS):
                        g = i * PAIRS + n
                        pe.wait_ge(mul_done, g + 1)
                        spread(c_bank, i, n, q, 1).then_inc(c_ready, 1)
                        if n:
                            add_states(i, n - 1)
                        pe.wait_ge(in_done, g + 1)
                        if n < PAIRS - 1:
                            spread(b_bank, i, n + 1, q, 0).then_inc(b_ready, 1)
                        else:
                            pe.wait_ge(parts_ready, 2 * (i + 2))
                            spread(b_bank, i, 0, 1 - q, 0).then_inc(b_ready, 1)
                            add_states(i, n)
                        if n == 1:
                            project_out(i, q)
                        if n == 3:
                            pe.wait_ge(x_added, i + 1)
                            transpose_xn(i + 1)
                        if n == 4:
                            conv(i + 1)
                        if n == 5:
                            project(i + 1, 1 - q)
            project_out(BATCH, 0)


_INS = ["L0_attn_hidden_states", "L0_attn_W_in", "L0_attn_W_xproj", "L0_attn_W_dt", "L0_attn_b_dt",
        "L0_attn_A_log", "L0_attn_D", "L0_attn_W_out", "L0_attn_K_x", "L0_attn_b_x", "L0_attn_K_z",
        "L0_attn_b_z", "L0_ffn_router_w", "L0_ffn_bias", "L0_ffn_gate_w", "L0_ffn_up_w", "L0_ffn_down_w",
        "L0_ffn_sh_gate_w", "L0_ffn_sh_up_w", "L0_ffn_sh_down_w"]
_COLUMNS = {"L0_attn_b_dt", "L0_attn_D", "L0_attn_b_x", "L0_attn_b_z"}


def kernel(**inputs):
    import concourse.bacc as _bacc
    from concourse.bass_utils import run_bass_kernel_spmd as _run

    nc = _bacc.Bacc("TRN2", target_bir_lowering=False, num_devices=1)
    arrays, args = {}, []
    for name in _INS:
        a = np.asarray(inputs[name])
        if name in _COLUMNS:
            a = a.reshape(P, 1)
        elif name in ("L0_attn_K_x", "L0_attn_K_z"):
            a = a.reshape(P * TAPS)
        elif name == "L0_ffn_router_w":
            a = a.T
        a = np.ascontiguousarray(a)
        arrays[f"in_{name}"] = a
        args.append(nc.dram_tensor(f"in_{name}", a.shape, mybir.dt.from_np(a.dtype), kind="ExternalInput").ap())
    args.append(nc.dram_tensor("out_0", (BATCH, SEQ, D), FP32, kind="ExternalOutput").ap())
    program(nc, *args)
    r = _run(nc, [arrays], core_ids=[0])
    return r.results[0]["out_0"]
```

```python
import numpy as np
import concourse.bass as bass
from concourse import mybir
from contextlib import ExitStack

FP32 = mybir.dt.float32
F32R = mybir.dt.float32r
BF16 = mybir.dt.bfloat16
ALU = mybir.AluOpType
ACT = mybir.ActivationFunctionType
AX = mybir.AxisListType

P = 128
D = 128
BATCH, SEQ = 8, 512
TT = SEQ // P
E, NSH = 16, 2
NE = E + NSH
GROUPS, TOP_EXPERTS, TOP_GROUPS = 4, 4, 2
EPG = E // GROUPS
ROUTE_SCALE = 2.5
NS, RANK, TAPS = 16, 8, 4
EPS = 1e-5
LAG = 3
PARTS = 3
PAIRS = NS // 2
LOG1P = (0.9999999698761054, -0.4999949309655034, 0.3331909588994792, -0.24842974904267215,
         0.19105978146072242, -0.13663184929591704, 0.07822523435688063, -0.029504798172988702,
         0.00523258431847857)
LN_STEPS = 2 * TT + 1


def run(pieces):
    for _ in pieces:
        pass


class Steps:

    def __init__(self, eng, sem, base):
        self.eng, self.sem, self.base, self.n = eng, sem, base, 0

    def do(self, ins):
        ins.then_inc(self.sem, 1)
        self.n += 1

    def settle(self):
        self.eng.wait_ge(self.sem, self.base + self.n)

    def settle_apart(self):
        self.settle()
        self.eng.sem_inc(self.sem, 1)
        self.n += 1


def program(nc, x_in, w_in, w_xproj, w_dt, b_dt, a_log, d_skip, w_out, k_x, b_x, k_z, b_z,
            router_w, route_bias, gate_w, up_w, down_w, sh_gate_w, sh_up_w, sh_down_w, out):
    ctx = ExitStack()
    with ctx:
        def sb(name, shape, dt=FP32):
            return ctx.enter_context(nc.sbuf_tensor(name, shape, dt))

        def sem(name):
            return ctx.enter_context(nc.semaphore(name))

        x_sb = sb("x_sb", [P, BATCH + 3, TT, D])
        ident = sb("ident", [P, P])
        ident_bf = sb("ident_bf", [P, P], BF16)
        w_hi = sb("w_hi", [P, NE, 3, P], F32R)
        w_lo = sb("w_lo", [P, NE, 3, P], F32R)
        stage = sb("stage", [P, NE, 3, P])
        xn = sb("xn", [P, TT, D])
        stats = sb("stats", [P, TT, 6])
        mean_var = sb("mean_var", [P, TT, 2])
        var_eps = sb("var_eps", [P, TT])
        rstd = sb("rstd", [P, TT])
        minus_half = sb("minus_half", [P, TT])
        bank = [ctx.enter_context(nc.psum_tensor(f"bank{n}", [P, 2, SEQ], FP32)) for n in range(4)]

        router_sb = sb("router_sb", [P, E])
        bias_sb = sb("bias_sb", [P, TT, E])
        sel_e = sb("sel_e", [P, E, P], BF16)
        before = sb("before", [P, GROUPS, GROUPS])
        same_tile = sb("same_tile", [P, TT, E])
        xt = sb("xt", [P, SEQ])
        x_hi = sb("x_hi", [P, SEQ], F32R)
        x_lo = sb("x_lo", [P, SEQ], F32R)
        sg = sb("sg", [P, 2, SEQ])
        act = sb("act", [P, 2, SEQ])
        act_hi = sb("act_hi", [P, 3, SEQ], F32R)
        act_lo = sb("act_lo", [P, 3, SEQ], F32R)
        out_t = sb("out_t", [P, SEQ])
        c_t = sb("c_t", [P, SEQ], BF16)
        c_parts = sb("c_parts", [P, TT, P], BF16)
        th = sb("th", [P, TT, E])
        score = sb("score", [P, TT, E])
        biased = sb("biased", [P, TT, E])
        pair_sum = sb("pair_sum", [P, TT * GROUPS, 6])
        g_score = sb("g_score", [P, TT, GROUPS])
        g_ge = sb("g_ge", [P, TT, GROUPS, GROUPS])
        g_gt = sb("g_gt", [P, TT, GROUPS, GROUPS])
        g_rank = sb("g_rank", [P, TT * GROUPS])
        g_in = sb("g_in", [P, TT * GROUPS])
        masked = sb("masked", [P, TT, E])
        top8 = sb("top8", [P, TT, 8])
        above = sb("above", [P, TT, E])
        tied = sb("tied", [P, TT, E])
        n_above = sb("n_above", [P, TT])
        tie_at = sb("tie_at", [P, TT, E])
        picked = sb("picked", [P, TT, E])
        total = sb("total", [P, TT])
        comb = sb("comb", [P, TT, E])
        rest = sb("rest", [P, TT, E])

        w_in_sb = sb("w_in_sb", [P, 2, P])
        taps_row = sb("taps_row", [P, 2, P, TAPS])
        w_tap = sb("w_tap", [P, 2, TAPS, P])
        w_xp = sb("w_xp", [P, RANK + 2 * NS])
        w_xp_t = sb("w_xp_t", [RANK, P])
        w_dt_sb = sb("w_dt_sb", [RANK, P])
        w_delta = sb("w_delta", [P, P])
        w_out_sb = sb("w_out_sb", [P, 2, D])
        b_x_sb = sb("b_x_sb", [P, 1])
        b_z_sb = sb("b_z_sb", [P, 1])
        b_dt_sb = sb("b_dt_sb", [P, 1])
        d_sb = sb("d_sb", [P, 1])
        a_log_sb = sb("a_log_sb", [P, NS])
        a_neg = sb("a_neg", [P, NS])
        sel_n = sb("sel_n", [P, 2 * NS, P], BF16)
        x_pad = sb("x_pad", [P, SEQ + TAPS - 1])
        u = [sb(f"u{n}", [P, SEQ]) for n in range(2)]
        z = [sb(f"z{n}", [P, SEQ]) for n in range(2)]
        delta = [sb(f"delta{n}", [P, SEQ]) for n in range(2)]
        du = [sb(f"du{n}", [P, SEQ]) for n in range(2)]
        bc_parts = [sb(f"bc_parts{n}", [P, SEQ], BF16) for n in range(2)]
        y_sb = sb("y_sb", [P, SEQ])

        setup = Setup(nc, ctx, dict(locals()))
        moe_phase(nc, ctx, "f1", dict(locals()), setup, None)
        mamba_phase(nc, ctx, dict(locals()), setup)
        moe_phase(nc, ctx, "f2", dict(locals()), None, out)


class Setup:

    CHUNKS = [(0, NSH)] + [(NSH + n, NSH + n + 4) for n in range(0, E, 4)]

    def __init__(self, nc, ctx, m):
        self.nc, self.m = nc, m

        def sem(name):
            return ctx.enter_context(nc.semaphore(name))

        self.x_first, self.x_rest = sem("x_first"), sem("x_rest")
        self.router_loaded, self.small_loaded = sem("router_loaded"), sem("small_loaded")
        self.experts_loaded = [sem(f"experts_loaded{n}") for n in range(len(self.CHUNKS))]
        self.idents, self.halves, self.selects = sem("idents"), sem("halves"), sem("selects")
        self.zeroed = sem("zeroed")
        self.hi_done, self.lo_done, self.taps_done = sem("hi_done"), sem("lo_done"), sem("taps_done")
        self.xp_pe, self.xp_act, self.a_step = sem("xp_pe"), sem("xp_act"), sem("a_step")

    def load(self, sp):
        m = self.m
        x_sb, stage, x_in = m["x_sb"], m["stage"], m["x_in"]
        sp.dma_start(x_sb[:, 1], x_in[0].rearrange("(t p) d -> p t d", p=P)).then_inc(self.x_first, 16)
        sp.dma_start(m["router_sb"][:, :], m["router_w"]).then_inc(self.router_loaded, 16)
        sp.dma_start(m["bias_sb"][:, :, :],
                     m["route_bias"].partition_broadcast(P).unsqueeze(1).broadcast_to([P, TT, E])
                     ).then_inc(self.router_loaded, 16)
        for (a, b), done in zip(self.CHUNKS, self.experts_loaded):
            if a == 0:
                srcs = (m["sh_gate_w"].rearrange("d (q f) -> d q f", q=NSH),
                        m["sh_up_w"].rearrange("d (q f) -> d q f", q=NSH),
                        m["sh_down_w"].rearrange("(q f) d -> f q d", q=NSH))
            else:
                srcs = [m[n][a - NSH:b - NSH].rearrange("e r c -> r e c") for n in ("gate_w", "up_w", "down_w")]
            for n, src in enumerate(srcs):
                sp.dma_start(stage[:, a:b, n, :], src).then_inc(done, 16)
        sp.dma_start(x_sb[:, 2:BATCH + 1], x_in[1:BATCH].rearrange("b (t p) d -> p b t d", p=P)
                     ).then_inc(self.x_rest, 16)
        small = [(m["w_in_sb"][:, :, :], m["w_in"].rearrange("d (h c) -> d h c", h=2)),
                 (m["taps_row"][:, 0].rearrange("p c k -> p (c k)"), m["k_x"].partition_broadcast(P)),
                 (m["taps_row"][:, 1].rearrange("p c k -> p (c k)"), m["k_z"].partition_broadcast(P)),
                 (m["w_xp"][:, :], m["w_xproj"]), (m["w_dt_sb"][:, :], m["w_dt"]),
                 (m["w_out_sb"][:, :, :], m["w_out"].rearrange("(h c) d -> c h d", h=2)),
                 (m["b_x_sb"][:, :], m["b_x"]), (m["b_z_sb"][:, :], m["b_z"]), (m["b_dt_sb"][:, :], m["b_dt"]),
                 (m["d_sb"][:, :], m["d_skip"]), (m["a_log_sb"][:, :], m["a_log"])]
        for dst, src in small:
            sp.dma_start(dst, src).then_inc(self.small_loaded, 16)
        self.small = 16 * len(small)

    def wait_small(self, eng):
        eng.wait_ge(self.small_loaded, self.small)

    def pool_first(self, pool):
        nc, m = self.nc, self.m
        for v in (m["ident"], m["ident_bf"]):
            nc.gpsimd.memset(v[:], 0.0).then_inc(self.idents, 1)
        nc.gpsimd.memset(m["before"][:], 1.0).then_inc(self.idents, 1)
        nc.gpsimd.memset(m["minus_half"][:], -0.5).then_inc(self.halves, 1)
        pool.wait_ge(self.idents, 3)
        for v in (m["ident"], m["ident_bf"]):
            nc.gpsimd.affine_select(out=v[:], in_=v[:], compare_op=ALU.not_equal, fill=1.0, base=0,
                                    pattern=[[-1, P]], channel_multiplier=1).then_inc(self.idents, 1)
        nc.gpsimd.affine_select(out=m["before"][:], in_=m["before"][:], compare_op=ALU.is_gt, fill=0.0, base=0,
                                pattern=[[1, GROUPS], [-1, GROUPS]], channel_multiplier=0).then_inc(self.idents, 1)
        pool.wait_ge(self.halves, 1)

    def pool_second(self, pool):
        nc, m = self.nc, self.m
        steps = Steps(pool, self.selects, 0)
        for v, rows in ((m["sel_e"], E), (m["sel_n"], 2 * NS)):
            steps.do(nc.gpsimd.memset(v[:], 0.0))
            for part in range(PARTS):
                steps.settle()
                steps.do(nc.gpsimd.affine_select(out=v[:], in_=v[:], compare_op=ALU.not_equal, fill=1.0,
                                                 base=-part * rows, pattern=[[-1, rows], [0, P]],
                                                 channel_multiplier=1))
        self.wait_small(pool)
        for h in range(2):
            for k in range(TAPS):
                nc.gpsimd.tensor_tensor(m["w_tap"][:, h, k, :], m["w_in_sb"][:, h, :], m["taps_row"][:, h, :, k],
                                        ALU.mult).then_inc(self.taps_done, 1)

    def act_high_parts(self, ae):
        for (a, b), done in zip(self.CHUNKS, self.experts_loaded):
            ae.wait_ge(done, 48)
            self.nc.scalar.activation(self.m["w_hi"][:, a:b], self.m["stage"][:, a:b], ACT.Copy
                                      ).then_inc(self.hi_done, 1)

    def dve_low_parts(self, dve):
        for n, (a, b) in enumerate(self.CHUNKS):
            dve.wait_ge(self.hi_done, n + 1)
            flat = lambda v: v[:, a:b].rearrange("p e n c -> p (e n c)")
            self.nc.vector.tensor_tensor(flat(self.m["w_lo"]), flat(self.m["stage"]),
                                         flat(self.m["w_hi"]).bitcast(FP32), ALU.subtract).then_inc(self.lo_done, 1)

    def dve_zeros(self, dve):
        nc, m = self.nc, self.m
        zero = Steps(dve, self.zeroed, 0)
        for v in (m["x_sb"][:, 0], m["x_sb"][:, BATCH + 1:], m["c_parts"][:], m["act_hi"][:].bitcast(FP32),
                  m["act_lo"][:].bitcast(FP32), m["x_pad"][:, 0:1], m["x_pad"][:, SEQ + 1:SEQ + TAPS - 1],
                  m["bc_parts"][0][:], m["bc_parts"][1][:], m["u"][1][:], m["z"][1][:], m["y_sb"][:]):
            zero.do(nc.vector.memset(v, 0.0))
        zero.do(nc.vector.memset(m["same_tile"][:], 1.0))
        zero.settle()
        zero.do(nc.vector.memset(m["same_tile"][:, :, 0:1], 0.0))
        zero.settle()

    def pe_delta_weight(self, pe, bank):
        nc, m = self.nc, self.m
        self.wait_small(pe)
        nc.tensor.transpose(bank[0:RANK, 0, 0:P], m["w_xp"][:, 0:RANK], m["ident"][:, :]).then_inc(self.xp_pe, 1)
        pe.wait_ge(self.xp_act, 1)
        nc.tensor.matmul(bank[:, 1, 0:P], m["w_xp_t"][:, :], m["w_dt_sb"][:, :], start=True,
                         stop=True).then_inc(self.xp_pe, 1)

    def act_delta_weight(self, ae, bank):
        nc, m = self.nc, self.m
        ae.wait_ge(self.xp_pe, 1)
        nc.scalar.activation(m["w_xp_t"][:, :], bank[0:RANK, 0, 0:P], ACT.Copy).then_inc(self.xp_act, 1)
        ae.wait_ge(self.xp_pe, 2)
        nc.scalar.activation(m["w_delta"][:, :], bank[:, 1, 0:P], ACT.Copy).then_inc(self.xp_act, 1)

    def act_decay_rates(self, ae):
        nc, m = self.nc, self.m
        nc.scalar.activation(m["a_neg"][:, :], m["a_log_sb"][:, :], ACT.Exp).then_inc(self.a_step, 1)
        ae.wait_ge(self.a_step, 1)
        nc.scalar.mul(m["a_neg"][:, :], m["a_neg"][:, :], -1.0).then_inc(self.a_step, 1)
        ae.wait_ge(self.a_step, 2)


def norm_stats(nc, steps, x_sb, slot, stats, mean_var, var_eps, ready):
    for t in range(TT):
        steps.do(nc.vector.bn_stats(stats[:, t, :], x_sb[:, slot, t, :]))
    yield
    steps.settle_apart()
    for t in range(TT):
        steps.do(nc.vector.bn_aggr(mean_var[:, t, :], stats[:, t, :]))
    steps.settle()
    nc.vector.tensor_scalar(var_eps[:, :], mean_var[:, :, 1], EPS, None, ALU.add).then_inc(ready, 1)
    yield


def norm_apply(nc, x_sb, slot, xn, mean_var, rstd, done):
    for t in range(TT):
        nc.vector.tensor_scalar(xn[:, t, :], x_sb[:, slot, t, :], mean_var[:, t, 0:1], rstd[:, t:t + 1],
                                ALU.subtract, ALU.mult).then_inc(done, 1)


def moe_phase(nc, ctx, tag, m, setup, out):
    (x_sb, ident, ident_bf, w_hi, w_lo, xn, stats, mean_var, var_eps, rstd, minus_half, bank, router_sb,
     bias_sb, sel_e, before, same_tile, xt, x_hi, x_lo, sg, act, act_hi, act_lo, out_t, c_t, c_parts, th,
     score, biased, pair_sum, g_score, g_ge, g_gt, g_rank, g_in, masked, top8, above, tied, n_above, tie_at,
     picked, total, comb, rest) = (m[n] for n in (
         "x_sb ident ident_bf w_hi w_lo xn stats mean_var var_eps rstd minus_half bank router_sb bias_sb "
         "sel_e before same_tile xt x_hi x_lo sg act act_hi act_lo out_t c_t c_parts th score biased "
         "pair_sum g_score g_ge g_gt g_rank g_in masked top8 above tied n_above tie_at picked total comb "
         "rest").split())
    h_bank, u_bank, c_bank = (bank[n] for n in range(3))
    acc, misc = bank[3][:, 0, :], bank[3][:, 1, :]
    misc_bf = misc.bitcast(BF16)

    def sem(name):
        return ctx.enter_context(nc.semaphore(f"{tag}_{name}"))

    h_ready, u_ready, cb_ready = sem("h_ready"), sem("u_ready"), sem("cb_ready")
    sg_ready = sem("sg_ready")
    w_done = sem("w_done")
    act_ready = sem("act_ready")
    hi_ready = sem("hi_ready")
    lo_ready = sem("lo_ready")
    down_done = sem("down_done")
    acc_read, ot_ready, x_added = sem("acc_read"), sem("ot_ready"), sem("x_added")
    var_ready, rstd_ready, xn_ready = sem("var_ready"), sem("rstd_ready"), sem("xn_ready")
    xt_ready, xt_copied, logits_ready, tanh_ready = (
        sem("xt_ready"), sem("xt_copied"), sem("logits_ready"), sem("tanh_ready"))
    parts_ready, ct_ready, ct_copied, x_split = (
        sem("parts_ready"), sem("ct_ready"), sem("ct_copied"), sem("x_split"))
    norm_step, route_step, stored = sem("norm_step"), sem("route_step"), sem("stored")
    ROUTE_STEPS = 34

    with nc.Block() as block:
        @block.sync
        def _(sp):
            if setup:
                setup.load(sp)
            if out is not None:
                rows = out.rearrange("b (t p) d -> b p t d", p=P)
                with sp.Fori(0, BATCH) as i:
                    sp.wait_ge(x_added, i + 2)
                    sp.dma_start(rows[i], x_sb[:, i + 1]).then_inc(stored, 16)
                sp.wait_ge(stored, 16 * BATCH)

        @block.gpsimd
        def _(pool):
            def norm_root(r):
                pool.wait_ge(var_ready, r + 1)
                nc.gpsimd.tensor_tensor(rstd[:, :], var_eps[:, :], minus_half[:, :], ALU.pow).then_inc(rstd_ready, 1)

            if setup:
                setup.pool_first(pool)
            norm_root(0)
            if setup:
                setup.pool_second(pool)
            with pool.Fori(0, BATCH) as i:
                for k in range(NE):
                    if k == 4:
                        norm_root(i + 1)
                    g = i * NE + k
                    pool.wait_ge(hi_ready, g + 1)
                    nc.gpsimd.tensor_tensor(act_lo[:, k % 3], act[:, k % 2], act_hi[:, k % 3].bitcast(FP32),
                                            ALU.subtract).then_inc(lo_ready, 1)

        @block.scalar
        def _(ae):
            nc.scalar.preload_act_table_set("silu_and_others")

            def copy_xt(r):
                ae.wait_ge(xt_ready, r + 1)
                nc.scalar.activation(xt[:, :], misc, ACT.Copy).then_inc(xt_copied, 1)

            def tanh(r):
                ae.wait_ge(logits_ready, r + 1)
                nc.scalar.activation(th[:].rearrange("p t e -> p (t e)"), misc[:, 0:TT * E], ACT.Tanh,
                                     scale=0.5).then_inc(tanh_ready, 1)

            def read_acc(i):
                nc.scalar.activation(out_t[:, :], acc, ACT.Copy, scale=0.5).then_inc(acc_read, 1)

            copy_xt(0)
            tanh(0)
            if setup:
                setup.act_high_parts(ae)
            with ae.Fori(0, BATCH) as i:
                for k in range(NE):
                    g = i * NE + k
                    if k == 1:
                        ae.wait_ge(ct_ready, i + 1)
                        nc.scalar.activation(c_t[:, :], misc_bf[:, 0:SEQ], ACT.Copy).then_inc(ct_copied, 1)
                    ae.wait_ge(h_ready, g + 1)
                    ae.wait_ge(act_ready, g + 1)
                    nc.scalar.activation(sg[:, k % 2], h_bank[:, k % 2], ACT.Silu).then_inc(sg_ready, 1)
                    for j in ([k - 1] if k else []) + ([k] if k == NE - 1 else []):
                        ae.wait_ge(act_ready, i * NE + j + 3)
                        ae.wait_ge(down_done, i * NE + j + LAG - 1)
                        nc.scalar.activation(act_hi[:, j % 3], act[:, j % 2], ACT.Copy).then_inc(hi_ready, 1)
                    if k == LAG:
                        ae.wait_ge(down_done, i * NE + LAG + 1)
                        read_acc(i)
                    if k == 6:
                        ae.wait_ge(x_split, 2 * i + 2)
                        copy_xt(i + 1)
                    if k == 8:
                        tanh(i + 1)
            if setup:
                setup.act_delta_weight(ae, c_bank)
            ae.wait_ge(down_done, BATCH * NE + LAG + 1)
            ae.wait_ge(ot_ready, BATCH)
            read_acc(BATCH)

        @block.vector
        def _(dve):
            dve.sem_inc(sg_ready, 2)
            dve.sem_inc(w_done, 2)
            dve.sem_inc(act_ready, 2)
            dve.sem_inc(lo_ready, LAG)
            dve.sem_inc(down_done, 1)

            def stats_of(r, slot):
                steps = Steps(dve, norm_step, r * LN_STEPS)
                return norm_stats(nc, steps, x_sb, slot, stats, mean_var, var_eps, var_ready)

            def apply_to(r, slot):
                dve.wait_ge(rstd_ready, r + 1)
                norm_apply(nc, x_sb, slot, xn, mean_var, rstd, xn_ready)

            def route(r, first=False):
                s = Steps(dve, route_step, r * ROUTE_STEPS)
                flat = lambda a: a[:].rearrange("p t e -> p (t e)")
                grouped = lambda a: a[:].rearrange("p t (g e) -> p (t g) e", g=GROUPS)
                gs = g_score[:].rearrange("p t g -> p (t g)")
                dve.wait_ge(tanh_ready, r + 1)
                s.do(nc.vector.tensor_scalar(flat(score), flat(th), 0.5, 0.5, ALU.mult, ALU.add))
                s.settle()
                s.do(nc.vector.tensor_tensor(flat(biased), flat(score), flat(bias_sb), ALU.add))
                s.settle()
                yield
                b4, at = grouped(biased), 0
                for gap in range(1, EPG):
                    n = EPG - gap
                    s.do(nc.vector.tensor_tensor(pair_sum[:, :, at:at + n], b4[:, :, 0:n], b4[:, :, gap:EPG],
                                                 ALU.add))
                    at += n
                s.settle()
                s.do(nc.vector.tensor_reduce(gs, pair_sum[:], AX.X, ALU.max))
                s.settle()
                yield
                other = g_score[:].unsqueeze(2).broadcast_to([P, TT, GROUPS, GROUPS])
                own = g_score[:].unsqueeze(3).broadcast_to([P, TT, GROUPS, GROUPS])
                s.do(nc.vector.tensor_tensor(g_ge[:], other, own, ALU.is_ge))
                s.do(nc.vector.tensor_tensor(g_gt[:], other, own, ALU.is_gt))
                s.settle()
                s.do(nc.vector.tensor_tensor(g_ge[:], g_ge[:],
                                             before[:].unsqueeze(1).broadcast_to([P, TT, GROUPS, GROUPS]),
                                             ALU.mult))
                s.settle()
                s.do(nc.vector.tensor_tensor(g_ge[:], g_ge[:], g_gt[:], ALU.max))
                s.settle()
                s.do(nc.vector.tensor_reduce(g_rank[:], g_ge[:].rearrange("p t g h -> p (t g) h"), AX.X, ALU.add))
                s.settle()
                yield
                s.do(nc.vector.tensor_scalar(g_in[:], g_rank[:], float(TOP_GROUPS), None, ALU.is_lt))
                s.settle()
                g_in_e = g_in[:].unsqueeze(2).broadcast_to([P, TT * GROUPS, EPG])
                s.do(nc.vector.tensor_tensor(grouped(masked), grouped(biased), g_in_e, ALU.mult))
                s.settle()
                s.do(nc.vector.scalar_tensor_tensor(grouped(masked), g_in_e, -1.0, grouped(masked),
                                                    ALU.add, ALU.add))
                yield
                s.settle_apart()
                for t in range(TT):
                    s.do(nc.vector.max(top8[:, t, :], masked[:, t, :]))
                s.settle()
                yield
                fourth = top8[:, :, TOP_EXPERTS - 1:TOP_EXPERTS].broadcast_to([P, TT, E])
                s.do(nc.vector.tensor_tensor(above[:], masked[:], fourth, ALU.is_gt))
                s.do(nc.vector.tensor_tensor(tied[:], masked[:], fourth, ALU.is_equal))
                s.settle()
                s.do(nc.vector.tensor_reduce(n_above[:], above[:], AX.X, ALU.add))
                s.do(nc.vector.tensor_tensor_scan(flat(tie_at), flat(same_tile), flat(tied), 0.0,
                                                  ALU.mult, ALU.add))
                s.settle()
                s.do(nc.vector.tensor_tensor(tie_at[:], tie_at[:],
                                             n_above[:].unsqueeze(2).broadcast_to([P, TT, E]), ALU.add))
                s.settle()
                s.do(nc.vector.scalar_tensor_tensor(flat(picked), flat(tie_at), float(TOP_EXPERTS), flat(tied),
                                                    ALU.is_le, ALU.mult))
                s.settle()
                yield
                s.do(nc.vector.tensor_tensor(picked[:], picked[:], above[:], ALU.add))
                s.settle()
                s.do(nc.vector.tensor_tensor(picked[:], picked[:], score[:], ALU.mult))
                s.settle()
                s.do(nc.vector.tensor_reduce(total[:], picked[:], AX.X, ALU.add))
                s.settle()
                yield
                s.do(nc.vector.tensor_scalar(total[:], total[:], 1e-20, None, ALU.add))
                s.settle()
                s.do(nc.vector.reciprocal(total[:], total[:]))
                s.settle()
                s.do(nc.vector.scalar_tensor_tensor(comb[:], picked[:], ROUTE_SCALE,
                                                    total[:].unsqueeze(2).broadcast_to([P, TT, E]),
                                                    ALU.mult, ALU.mult))
                s.settle()
                yield
                if not first:
                    dve.wait_ge(ct_ready, r)
                s.do(nc.vector.tensor_copy(c_parts[:, :, 0:E], comb[:]))
                s.settle()
                s.do(nc.vector.tensor_tensor(rest[:], comb[:], c_parts[:, :, 0:E], ALU.subtract))
                s.settle()
                s.do(nc.vector.tensor_copy(c_parts[:, :, E:2 * E], rest[:]))
                s.settle()
                nc.vector.tensor_tensor(c_parts[:, :, 2 * E:3 * E], rest[:], c_parts[:, :, E:2 * E],
                                        ALU.subtract).then_inc(parts_ready, 1)
                assert s.n == ROUTE_STEPS, s.n
                yield

            def split_x(r):
                dve.wait_ge(xt_copied, r + 1)
                nc.vector.tensor_copy(x_hi[:, :], xt[:, :]).then_inc(x_split, 1)
                dve.wait_ge(x_split, 2 * r + 1)
                nc.vector.tensor_tensor(x_lo[:, :], xt[:, :], x_hi[:, :].bitcast(FP32),
                                        ALU.subtract).then_inc(x_split, 1)

            def add_rows(i):
                dve.wait_ge(ot_ready, i + 1)
                nc.vector.tensor_tensor(x_sb[:, i], x_sb[:, i], misc.rearrange("p (t d) -> p t d", t=TT),
                                        ALU.add).then_inc(x_added, 1)

            if setup:
                dve.wait_ge(setup.x_first, 16)
            run(stats_of(0, 1))
            if setup:
                setup.dve_zeros(dve)
            apply_to(0, 1)
            if setup:
                dve.wait_ge(setup.router_loaded, 32)
                dve.wait_ge(setup.idents, 6)
            split_x(0)
            run(route(0, first=True))
            if setup:
                setup.dve_low_parts(dve)
                dve.wait_ge(setup.x_rest, 16)
            with dve.Fori(0, BATCH) as i:
                norming, routing = stats_of(i + 1, i + 2), route(i + 1)
                for k in range(NE):
                    g = i * NE + k
                    dve.wait_ge(sg_ready, g + 3)
                    if k >= NSH:
                        r = i * E + (k - NSH)
                        dve.wait_ge(cb_ready, r + 1)
                        nc.vector.tensor_tensor(sg[:, k % 2], sg[:, k % 2], c_bank[:, k % 2],
                                                ALU.mult).then_inc(w_done, 1)
                    dve.wait_ge(u_ready, g + 1)
                    if k == NE - 1:
                        split_x(i + 1)
                    if k >= NSH:
                        dve.wait_ge(w_done, r + 3)
                    dve.wait_ge(lo_ready, g + LAG - 1)
                    nc.vector.tensor_tensor(act[:, k % 2], sg[:, k % 2], u_bank[:, k % 2],
                                            ALU.mult).then_inc(act_ready, 1)
                    if k in (2, 3):
                        next(norming)
                    if k == 5:
                        add_rows(i)
                    if k == 5:
                        dve.wait_ge(xt_ready, i + 1)
                        apply_to(i + 1, i + 2)
                    if 9 <= k <= 17:
                        next(routing)
            add_rows(BATCH)
            dve.wait_ge(x_added, BATCH + 1)

        @block.tensor
        def _(pe):
            def transpose_xn(r):
                pe.wait_ge(xn_ready, TT * (r + 1))
                for t in range(TT):
                    last = nc.tensor.transpose(misc[:, t * P:(t + 1) * P], xn[:, t, :], ident[:, :])
                last.then_inc(xt_ready, 1)

            def logits(r):
                pe.wait_ge(xt_copied, r + 1)
                for t in range(TT):
                    last = nc.tensor.matmul(misc[:, t * E:(t + 1) * E], xt[:, t * P:(t + 1) * P],
                                            router_sb[:, :], start=True, stop=True)
                last.then_inc(logits_ready, 1)

            def transpose_parts(r):
                pe.wait_ge(tanh_ready, r + 1)
                pe.wait_ge(parts_ready, r + 1)
                for t in range(TT):
                    last = nc.tensor.transpose(misc_bf[:, t * P:(t + 1) * P], c_parts[:, t, :], ident_bf[:, :])
                last.then_inc(ct_ready, 1)

            def down(i, k):
                j = k % NE
                pe.wait_ge(lo_ready, i * NE + k + 1 + LAG)
                if k == 0:
                    pe.wait_ge(acc_read, i + 1)
                dt = w_hi[:, j, 2, :], w_lo[:, j, 2, :]
                first, last = j == 0, j == NE - 1
                nc.tensor.matmul(acc, dt[0], act_hi[:, j % 3], start=first, stop=False, skip_group_check=True)
                nc.tensor.matmul(acc, dt[1], act_hi[:, j % 3], start=False, stop=False, skip_group_check=True)
                nc.tensor.matmul(acc, dt[0], act_lo[:, j % 3], start=False, stop=last,
                                 skip_group_check=True).then_inc(down_done, 1)

            def transpose_out(i):
                pe.wait_ge(acc_read, i + 1)
                for t in range(TT):
                    last = nc.tensor.transpose(misc[:, t * P:(t + 1) * P], out_t[:, t * P:(t + 1) * P], ident[:, :])
                last.then_inc(ot_ready, 1)

            def product(dst, n, k, new_row=None):
                if new_row is not None:
                    pe.wait_ge(x_split, 2 * new_row + 1)
                nc.tensor.matmul(dst, w_hi[:, k, n, :], x_hi[:, :], start=True, stop=False)
                nc.tensor.matmul(dst, w_lo[:, k, n, :], x_hi[:, :], start=False, stop=False)
                if new_row is not None:
                    pe.wait_ge(x_split, 2 * new_row + 2)
                return nc.tensor.matmul(dst, w_hi[:, k, n, :], x_lo[:, :], start=False, stop=True)

            if setup:
                pe.wait_ge(setup.idents, 6)
            transpose_xn(0)
            if setup:
                pe.wait_ge(setup.router_loaded, 32)
            logits(0)
            if setup:
                pe.wait_ge(setup.zeroed, 1)
                pe.wait_ge(setup.lo_done, len(setup.CHUNKS))
                pe.wait_ge(setup.selects, 8)
            nc.tensor.matmul(acc, w_hi[:, 0, 2, :], act_hi[:, 1], start=True, stop=True)
            with pe.Fori(0, BATCH) as i:
                for k in range(NE):
                    g = i * NE + k
                    if k < LAG:
                        down(i, k - LAG)
                    pe.wait_ge(sg_ready, g + 1)
                    product(h_bank[:, k % 2], 0, k, i if k == 0 else None).then_inc(h_ready, 1)
                    pe.wait_ge(act_ready, g + 1)
                    product(u_bank[:, k % 2], 1, k).then_inc(u_ready, 1)
                    if k == 0:
                        transpose_parts(i)
                    if k >= NSH:
                        r = i * E + (k - NSH)
                        pe.wait_ge(ct_copied, i + 1)
                        pe.wait_ge(w_done, r + 1)
                        nc.tensor.matmul(c_bank[:, k % 2], sel_e[:, k - NSH, :], c_t[:, :], start=True,
                                         stop=True).then_inc(cb_ready, 1)
                    if k >= LAG:
                        down(i, k - LAG)
                    if k == 4:
                        pe.wait_ge(ct_copied, i + 1)
                        transpose_out(i)
                    if k == 6:
                        pe.wait_ge(x_added, i + 1)
                        transpose_xn(i + 1)
                    if k == 8:
                        logits(i + 1)
            if setup:
                pe.wait_ge(w_done, BATCH * E + 2)
                setup.pe_delta_weight(pe, c_bank)
            for k in range(-LAG, 0):
                down(BATCH, k)
            transpose_out(BATCH)


def mamba_phase(nc, ctx, m, setup):
    (x_sb, ident, xn, stats, mean_var, var_eps, rstd, minus_half, bank, w_tap, w_xp, w_delta, w_out_sb,
     b_x_sb, b_z_sb, b_dt_sb, d_sb, a_neg, sel_n, x_pad, u, z, delta, du, bc_parts, y_sb, stage) = (
        m[n] for n in (
            "x_sb ident xn stats mean_var var_eps rstd minus_half bank w_tap w_xp w_delta w_out_sb b_x_sb "
            "b_z_sb b_dt_sb d_sb a_neg sel_n x_pad u z delta du bc_parts y_sb stage").split())
    b_bank, c_bank = bank[0], bank[1]
    y_acc, misc = bank[2][:, 0, :], bank[2][:, 1, :]
    front = bank[3]

    room = stage[:].rearrange("p a b c -> p (a b c)")
    at = [0]

    def place(*shape):
        n = int(np.prod(shape))
        at[0] += n
        v = room[:, at[0] - n:at[0]]
        return v.rearrange("p (a s l) -> p a s l", a=shape[0], s=shape[1]) if len(shape) == 3 else (
            v.rearrange("p (s l) -> p s l", s=shape[0]) if len(shape) == 2 else v)

    decay = place(2, 2, SEQ)
    state_in = place(2, SEQ)
    state = place(2, SEQ)
    state_c = place(2, 2, SEQ)
    soft_abs, soft_relu, soft_e = m["sg"][:, 0], m["sg"][:, 1], m["act"][:, 0]
    soft_q, rest, second = m["out_t"][:, :], m["xt"][:, :], m["c_t"][:, :]
    assert at[0] <= NE * 3 * P

    def sem(name):
        return ctx.enter_context(nc.semaphore(f"mb_{name}"))

    var_ready, rstd_ready, xn_ready, norm_step = (
        sem("var_ready"), sem("rstd_ready"), sem("xn_ready"), sem("norm_step"))
    xt_ready, xt_copied, conv_ready, gated = sem("xt_ready"), sem("xt_copied"), sem("conv_ready"), sem("gated")
    bc_ready, dt_ready = sem("bc_ready"), sem("dt_ready")
    first_part, rest_ready, second_part, parts_ready = (
        sem("first_part"), sem("rest_ready"), sem("second_part"), sem("parts_ready"))
    soft_act, soft_dve, du_ready = sem("soft_act"), sem("soft_dve"), sem("du_ready")
    b_ready, c_ready, decay_ready = sem("b_ready"), sem("c_ready"), sem("decay_ready")
    in_done = sem("in_done")
    scan_done = sem("scan_done")
    mul_done = sem("mul_done")
    sum_done = sem("sum_done")
    out_ready = sem("out_ready")
    x_added = sem("x_added")
    y_ready, pair_added, zeroed = sem("y_ready"), sem("pair_added"), sem("zeroed")
    ACT_SOFT, DVE_SOFT = 3, 10

    with nc.Block() as block:
        @block.gpsimd
        def _(pool):
            def norm_root(r):
                pool.wait_ge(var_ready, r + 1)
                nc.gpsimd.tensor_tensor(rstd[:, :], var_eps[:, :], minus_half[:, :], ALU.pow).then_inc(rstd_ready, 1)

            norm_root(0)
            norm_root(1)
            with pool.Fori(0, BATCH) as i:
                for n in range(PAIRS):
                    pool.wait_ge(mul_done, i * PAIRS + n + 2)
                    both = state_c[:, n % 2]
                    nc.gpsimd.tensor_tensor(both[:, 0], both[:, 0], both[:, 1], ALU.add).then_inc(pair_added, 1)
                    if n == 5:
                        norm_root(i + 2)

        @block.scalar
        def _(ae):
            def copy_xt(r):
                ae.wait_ge(xt_ready, r + 1)
                nc.scalar.activation(x_pad[:, 1:SEQ + 1], misc, ACT.Copy).then_inc(xt_copied, 1)

            def gelu(r, h, dst, bias):
                ae.wait_ge(conv_ready, 2 * r + 1 + h)
                nc.scalar.activation(dst[:, :], front[:, h, :], ACT.Gelu, bias=bias[:, 0:1]).then_inc(gated, 1)
                nc.scalar.preload_act_table_set("exp_and_others")

            def parts(r, q):
                ae.wait_ge(bc_ready, r + 1)
                nc.scalar.activation(bc_parts[q][0:2 * NS, :], front[0:2 * NS, 0, :], ACT.Copy).then_inc(first_part, 1)
                ae.wait_ge(rest_ready, r + 1)
                nc.scalar.activation(second[0:2 * NS, :], rest[0:2 * NS, :], ACT.Copy).then_inc(second_part, 1)
                nc.scalar.activation(bc_parts[q][2 * NS:4 * NS, :], rest[0:2 * NS, :], ACT.Copy).then_inc(parts_ready, 1)

            def soft(r):
                base = r * ACT_SOFT
                ae.wait_ge(dt_ready, r + 1)
                nc.scalar.activation(soft_abs, front[:, 1, :], ACT.Abs, bias=b_dt_sb[:, 0:1]).then_inc(soft_act, 1)
                nc.scalar.activation(soft_relu, front[:, 1, :], ACT.Relu, bias=b_dt_sb[:, 0:1]).then_inc(soft_act, 1)
                ae.wait_ge(soft_act, base + 2)
                nc.scalar.activation(soft_e, soft_abs, ACT.Exp, scale=-1.0).then_inc(soft_act, 1)

            def decays(i, n, q):
                ae.wait_ge(scan_done, i * PAIRS + n + 1)
                if n == 0:
                    ae.wait_ge(soft_dve, (i + 1) * DVE_SOFT)
                for s in range(2):
                    nc.scalar.activation(decay[:, n % 2, s, 1:SEQ], delta[q][:, 1:SEQ], ACT.Exp,
                                         scale=a_neg[:, 2 * n + s:2 * n + s + 1]).then_inc(decay_ready, 1)

            setup.act_decay_rates(ae)
            copy_xt(0)
            gelu(0, 0, u[0], b_x_sb)
            soft(0)
            parts(0, 0)
            gelu(0, 1, z[0], b_z_sb)
            copy_xt(1)
            ae.wait_ge(zeroed, 3)
            decays(0, 0, 0)
            with ae.Fori(0, BATCH // 2) as turn:
                for q in range(2):
                    i = turn * 2 + q
                    for n in range(PAIRS):
                        if n < PAIRS - 1:
                            decays(i, n + 1, q)
                        else:
                            decays(i + 1, 0, 1 - q)
                        if n == 2:
                            ae.wait_ge(y_ready, i + 1)
                            gelu(i + 1, 0, u[1 - q], b_x_sb)
                        if n == 3:
                            ae.wait_ge(soft_dve, (i + 1) * DVE_SOFT)
                            soft(i + 1)
                        if n == 4:
                            parts(i + 1, 1 - q)
                        if n == 7:
                            ae.wait_ge(out_ready, i + 2)
                            gelu(i + 1, 1, z[1 - q], b_z_sb)
                            copy_xt(i + 2)

        @block.vector
        def _(dve):
            def stats_of(r, slot):
                steps = Steps(dve, norm_step, r * LN_STEPS)
                return norm_stats(nc, steps, x_sb, slot, stats, mean_var, var_eps, var_ready)

            def apply_to(r, slot):
                dve.wait_ge(rstd_ready, r + 1)
                norm_apply(nc, x_sb, slot, xn, mean_var, rstd, xn_ready)

            def parts(r, q):
                dve.wait_ge(first_part, r + 1)
                nc.vector.tensor_tensor(rest[0:2 * NS, :], front[0:2 * NS, 0, :], bc_parts[q][0:2 * NS, :],
                                        ALU.subtract).then_inc(rest_ready, 1)
                dve.wait_ge(second_part, r + 1)
                nc.vector.tensor_tensor(bc_parts[q][4 * NS:6 * NS, :], rest[0:2 * NS, :], second[0:2 * NS, :],
                                        ALU.subtract).then_inc(parts_ready, 1)

            def soft(r, q):
                count = Steps(dve, soft_dve, r * DVE_SOFT)

                def step(ins):
                    count.do(ins)
                    count.settle()

                dve.wait_ge(soft_act, (r + 1) * ACT_SOFT)
                step(nc.vector.tensor_scalar(soft_q, soft_e, LOG1P[-1], LOG1P[-2], ALU.mult, ALU.add))
                step(nc.vector.tensor_tensor(soft_q, soft_q, soft_e, ALU.mult))
                for c in LOG1P[-3::-1]:
                    step(nc.vector.scalar_tensor_tensor(soft_q, soft_q, c, soft_e, ALU.add, ALU.mult))
                step(nc.vector.tensor_tensor(delta[q][:, :], soft_q, soft_relu, ALU.add))
                assert count.n == DVE_SOFT
                nc.vector.tensor_tensor(du[q][:, :], delta[q][:, :], u[q][:, :], ALU.mult).then_inc(du_ready, 1)

            dve.sem_inc(scan_done, 2)
            for credited in (mul_done, sum_done, out_ready, x_added):
                dve.sem_inc(credited, 1)
            for v in (decay[:, 0, :, 0:1], decay[:, 1, :, 0:1], y_acc):
                nc.vector.memset(v, 0.0).then_inc(zeroed, 1)
            run(stats_of(0, 1))
            apply_to(0, 1)
            run(stats_of(1, 2))
            dve.wait_ge(xt_ready, 1)
            apply_to(1, 2)
            parts(0, 0)
            soft(0, 0)
            with dve.Fori(0, BATCH // 2) as turn:
                for q in range(2):
                    i = turn * 2 + q
                    for n in range(PAIRS):
                        g = i * PAIRS + n
                        dve.wait_ge(b_ready, g + 1)
                        if n == 0:
                            dve.wait_ge(du_ready, i + 1)
                        dve.wait_ge(scan_done, g + 2)
                        nc.vector.tensor_tensor(state_in, du[q][:, :].unsqueeze(1).broadcast_to([P, 2, SEQ]),
                                                b_bank[:], ALU.mult).then_inc(in_done, 1)
                        dve.wait_ge(decay_ready, 2 * g + 2)
                        dve.wait_ge(in_done, g + 1)
                        dve.wait_ge(mul_done, g + 1)
                        nc.vector.tensor_tensor_scan(
                            state.rearrange("p s l -> p (s l)"), decay[:, n % 2].rearrange("p s l -> p (s l)"),
                            state_in.rearrange("p s l -> p (s l)"), 0.0, ALU.mult, ALU.add).then_inc(scan_done, 1)
                        dve.wait_ge(c_ready, g + 1)
                        dve.wait_ge(scan_done, g + 3)
                        if n >= 2:
                            dve.wait_ge(sum_done, g)
                        nc.vector.tensor_tensor(state_c[:, n % 2], state, c_bank[:], ALU.mult).then_inc(mul_done, 1)
                        if n == 0:
                            dve.wait_ge(sum_done, i * PAIRS + 1)
                            dve.wait_ge(out_ready, i + 1)
                            nc.vector.scalar_tensor_tensor(y_sb[:, :], u[1 - q][:, :], d_sb[:, 0:1], y_acc,
                                                           ALU.mult, ALU.add).then_inc(y_ready, 1)
                        if n == 4:
                            parts(i + 1, 1 - q)
                        if n == 5:
                            dve.wait_ge(out_ready, i + 2)
                            nc.vector.tensor_tensor(x_sb[:, i], x_sb[:, i],
                                                    misc.rearrange("p (t d) -> p t d", t=TT),
                                                    ALU.add).then_inc(x_added, 1)
                            soft(i + 1, 1 - q)
                            run(stats_of(i + 2, i + 3))
                        if n == 6:
                            dve.wait_ge(xt_ready, i + 2)
                            apply_to(i + 2, i + 3)
            dve.wait_ge(sum_done, BATCH * PAIRS + 1)
            dve.wait_ge(out_ready, BATCH + 1)
            nc.vector.scalar_tensor_tensor(y_sb[:, :], u[1][:, :], d_sb[:, 0:1], y_acc, ALU.mult,
                                           ALU.add).then_inc(y_ready, 1)
            dve.wait_ge(out_ready, BATCH + 2)
            nc.vector.tensor_tensor(x_sb[:, BATCH], x_sb[:, BATCH], misc.rearrange("p (t d) -> p t d", t=TT),
                                    ALU.add).then_inc(x_added, 1)
            dve.wait_ge(x_added, BATCH + 2)

        @block.tensor
        def _(pe):
            def transpose_xn(r):
                pe.wait_ge(x_added, r)
                pe.wait_ge(xn_ready, TT * (r + 1))
                for t in range(TT):
                    last = nc.tensor.transpose(misc[:, t * P:(t + 1) * P], xn[:, t, :], ident[:, :])
                last.then_inc(xt_ready, 1)

            def conv(r, h, taps):
                pe.wait_ge(xt_copied, r + 1)
                for k in taps:
                    last = nc.tensor.matmul(front[:, h, :], w_tap[:, h, k, :], x_pad[:, k:k + SEQ],
                                            start=(k == 0), stop=(k == TAPS - 1))
                if TAPS - 1 in taps:
                    last.then_inc(conv_ready, 1)

            def project_bc(r, q):
                pe.wait_ge(gated, 2 * r + 1)
                nc.tensor.matmul(front[0:2 * NS, 0, :], w_xp[:, RANK:], u[q][:, :], start=True,
                                 stop=True).then_inc(bc_ready, 1)

            def project_delta(r, q):
                nc.tensor.matmul(front[:, 1, :], w_delta[:, :], u[q][:, :], start=True,
                                 stop=True).then_inc(dt_ready, 1)

            def spread(dst, i, n, q, c):
                for s in range(2):
                    last = nc.tensor.matmul(dst[:, s, :], sel_n[:, c * NS + 2 * n + s, :], bc_parts[q][:, :],
                                            start=True, stop=True)
                return last

            def add_states(i, n):
                pe.wait_ge(pair_added, i * PAIRS + n + 1)
                if n == 0:
                    pe.wait_ge(y_ready, i + 1)
                nc.tensor.matmul(y_acc, ident[:, :], state_c[:, n % 2, 0, :], start=(n == 0),
                                 stop=(n == PAIRS - 1)).then_inc(sum_done, 1)

            def project_out(i, q, tiles):
                pe.wait_ge(y_ready, i + 1)
                for t in tiles:
                    cols = slice(t * P, (t + 1) * P)
                    nc.tensor.matmul(misc[:, cols], y_sb[:, cols], w_out_sb[:, 0, :], start=True, stop=False)
                    last = nc.tensor.matmul(misc[:, cols], z[1 - q][:, cols], w_out_sb[:, 1, :], start=False,
                                            stop=True)
                if TT - 1 in tiles:
                    last.then_inc(out_ready, 1)

            setup.wait_small(pe)
            pe.wait_ge(setup.taps_done, 2 * TAPS)
            pe.wait_ge(zeroed, 1)
            transpose_xn(0)
            conv(0, 0, range(TAPS))
            project_bc(0, 0)
            project_delta(0, 0)
            pe.wait_ge(soft_act, 2)
            conv(0, 1, range(TAPS))
            transpose_xn(1)
            pe.wait_ge(parts_ready, 2)
            spread(b_bank, 0, 0, 0, 0).then_inc(b_ready, 1)
            pe.wait_ge(zeroed, 3)
            with pe.Fori(0, BATCH // 2) as turn:
                for q in range(2):
                    i = turn * 2 + q
                    first = {1: lambda: conv(i + 1, 0, [1]), 2: lambda: conv(i + 1, 0, [3]),
                             3: lambda: project_bc(i + 1, 1 - q), 4: lambda: project_out(i, q, [0, 1]),
                             5: lambda: conv(i + 1, 1, [0]), 6: lambda: conv(i + 1, 1, [2]),
                             7: lambda: transpose_xn(i + 2)}
                    second = {0: lambda: conv(i + 1, 0, [0]), 1: lambda: conv(i + 1, 0, [2]),
                              3: lambda: project_delta(i + 1, 1 - q), 4: lambda: project_out(i, q, [2, 3]),
                              5: lambda: conv(i + 1, 1, [1]), 6: lambda: conv(i + 1, 1, [3])}
                    for n in range(PAIRS):
                        g = i * PAIRS + n
                        pe.wait_ge(mul_done, g + 1)
                        spread(c_bank, i, n, q, 1).then_inc(c_ready, 1)
                        if n == 4:
                            pe.wait_ge(xt_copied, i + 2)
                        if n == 5:
                            pe.wait_ge(soft_act, (i + 1) * ACT_SOFT + 2)
                        if n in first:
                            first[n]()
                        pe.wait_ge(in_done, g + 1)
                        if n < PAIRS - 1:
                            spread(b_bank, i, n + 1, q, 0).then_inc(b_ready, 1)
                        else:
                            pe.wait_ge(parts_ready, 2 * (i + 2))
                            spread(b_bank, i, 0, 1 - q, 0).then_inc(b_ready, 1)
                        if n in second:
                            second[n]()
                        if n:
                            add_states(i, n - 1)
                    add_states(i, PAIRS - 1)
            pe.wait_ge(xt_copied, BATCH + 2)
            project_out(BATCH, 0, range(TT))


_INS = ["L0_attn_hidden_states", "L0_attn_W_in", "L0_attn_W_xproj", "L0_attn_W_dt", "L0_attn_b_dt",
        "L0_attn_A_log", "L0_attn_D", "L0_attn_W_out", "L0_attn_K_x", "L0_attn_b_x", "L0_attn_K_z",
        "L0_attn_b_z", "L0_ffn_router_w", "L0_ffn_bias", "L0_ffn_gate_w", "L0_ffn_up_w", "L0_ffn_down_w",
        "L0_ffn_sh_gate_w", "L0_ffn_sh_up_w", "L0_ffn_sh_down_w"]
_COLUMNS = {"L0_attn_b_dt", "L0_attn_D", "L0_attn_b_x", "L0_attn_b_z"}


def kernel(**inputs):
    import concourse.bacc as _bacc
    from concourse.bass_utils import run_bass_kernel_spmd as _run

    nc = _bacc.Bacc("TRN2", target_bir_lowering=False, num_devices=1)
    arrays, args = {}, []
    for name in _INS:
        a = np.asarray(inputs[name])
        if name in _COLUMNS:
            a = a.reshape(P, 1)
        elif name in ("L0_attn_K_x", "L0_attn_K_z"):
            a = a.reshape(P * TAPS)
        elif name == "L0_ffn_router_w":
            a = a.T
        a = np.ascontiguousarray(a)
        arrays[f"in_{name}"] = a
        args.append(nc.dram_tensor(f"in_{name}", a.shape, mybir.dt.from_np(a.dtype), kind="ExternalInput").ap())
    args.append(nc.dram_tensor("out_0", (BATCH, SEQ, D), FP32, kind="ExternalOutput").ap())
    program(nc, *args)
    r = _run(nc, [arrays], core_ids=[0])
    return r.results[0]["out_0"]
```

```python
import numpy as np
import concourse.bass as bass
from concourse import mybir
from contextlib import ExitStack

FP32 = mybir.dt.float32
F32R = mybir.dt.float32r
BF16 = mybir.dt.bfloat16
ALU = mybir.AluOpType
ACT = mybir.ActivationFunctionType
AX = mybir.AxisListType

P = 128
D = 128
BATCH, SEQ = 8, 512
TT = SEQ // P
E, NSH = 16, 2
NE = E + NSH
GROUPS, TOP_EXPERTS, TOP_GROUPS = 4, 4, 2
EPG = E // GROUPS
ROUTE_SCALE = 2.5
NS, RANK, TAPS = 16, 8, 4
EPS = 1e-5
LAG = 3
PARTS = 3
PAIRS = NS // 2
LOG1P = ((1.009357526868805, 1.1060679102671753), (-0.08225465651132796, 3.2574848537500833),
         (-1.4247416849819245, 2.7021171047885773), (-2.3216944609803276, 0.4324090385033215))
LOG1P_SCALE = 0.00523258431847857
LN_STEPS = 2 * TT + 1


def run(pieces):
    for _ in pieces:
        pass


class Steps:

    def __init__(self, eng, sem, base):
        self.eng, self.sem, self.base, self.n = eng, sem, base, 0

    def do(self, ins):
        ins.then_inc(self.sem, 1)
        self.n += 1

    def settle(self):
        self.eng.wait_ge(self.sem, self.base + self.n)

    def settle_apart(self):
        self.settle()
        self.eng.sem_inc(self.sem, 1)
        self.n += 1


def program(nc, x_in, w_in, w_xproj, w_dt, b_dt, a_log, d_skip, w_out, k_x, b_x, k_z, b_z,
            router_w, route_bias, gate_w, up_w, down_w, sh_gate_w, sh_up_w, sh_down_w, out):
    ctx = ExitStack()
    with ctx:
        def sb(name, shape, dt=FP32):
            return ctx.enter_context(nc.sbuf_tensor(name, shape, dt))

        def sem(name):
            return ctx.enter_context(nc.semaphore(name))

        x_sb = sb("x_sb", [P, BATCH + 3, TT, D])
        ident = sb("ident", [P, P])
        ident_bf = sb("ident_bf", [P, P], BF16)
        w_hi = sb("w_hi", [P, NE, 3, P], F32R)
        w_lo = sb("w_lo", [P, NE, 3, P], F32R)
        stage = sb("stage", [P, NE, 3, P])
        xn = sb("xn", [P, TT, D])
        stats = sb("stats", [P, TT, 6])
        mean_var = sb("mean_var", [P, TT, 2])
        var_eps = sb("var_eps", [P, TT])
        rstd = sb("rstd", [P, TT])
        minus_half = sb("minus_half", [P, TT])
        bank = [ctx.enter_context(nc.psum_tensor(f"bank{n}", [P, 2, SEQ], FP32)) for n in range(4)]

        router_sb = sb("router_sb", [P, E])
        bias_sb = sb("bias_sb", [P, TT, E])
        sel_e_row = sb("sel_e_row", [P, E], BF16)
        sel_n_row = sb("sel_n_row", [P, 2 * NS], BF16)
        sel_e = sb("sel_e", [P, E, P], BF16)
        before = sb("before", [P, GROUPS, GROUPS])
        same_tile = sb("same_tile", [P, TT, E])
        xt = sb("xt", [P, SEQ])
        sg = sb("sg", [P, 2, SEQ])
        act = sb("act", [P, 2, SEQ])
        act_hi = sb("act_hi", [P, 3, SEQ], F32R)
        act_lo = sb("act_lo", [P, 3, SEQ], F32R)
        out_t = sb("out_t", [P, SEQ])
        c_t = sb("c_t", [P, SEQ], BF16)
        c_parts = sb("c_parts", [P, TT, P], BF16)
        th = sb("th", [P, TT, E])
        score = sb("score", [P, TT, E])
        biased = sb("biased", [P, TT, E])
        pair_sum = sb("pair_sum", [P, TT * GROUPS, 6])
        g_score = sb("g_score", [P, TT, GROUPS])
        g_ge = sb("g_ge", [P, TT, GROUPS, GROUPS])
        g_gt = sb("g_gt", [P, TT, GROUPS, GROUPS])
        g_rank = sb("g_rank", [P, TT * GROUPS])
        g_in = sb("g_in", [P, TT * GROUPS])
        masked = sb("masked", [P, TT, E])
        top8 = sb("top8", [P, TT, 8])
        above = sb("above", [P, TT, E])
        tied = sb("tied", [P, TT, E])
        n_above = sb("n_above", [P, TT])
        tie_at = sb("tie_at", [P, TT, E])
        picked = sb("picked", [P, TT, E])
        total = sb("total", [P, TT])
        comb = sb("comb", [P, TT, E])
        rest = sb("rest", [P, TT, E])

        w_in_sb = sb("w_in_sb", [P, 2, P])
        taps_row = sb("taps_row", [P, 2, P, TAPS])
        w_tap = sb("w_tap", [P, 2, TAPS, P])
        w_xp = sb("w_xp", [P, RANK + 2 * NS])
        w_xp_t = sb("w_xp_t", [RANK, P])
        w_dt_sb = sb("w_dt_sb", [RANK, P])
        w_delta = sb("w_delta", [P, P])
        w_out_sb = sb("w_out_sb", [P, 2, D])
        b_x_sb = sb("b_x_sb", [P, 1])
        b_z_sb = sb("b_z_sb", [P, 1])
        b_dt_sb = sb("b_dt_sb", [P, 1])
        d_sb = sb("d_sb", [P, 1])
        a_log_sb = sb("a_log_sb", [P, NS])
        a_neg = sb("a_neg", [P, NS])
        log_consts = sb("log_consts", [P, 2 * len(LOG1P)])
        sel_n = sb("sel_n", [P, 2 * NS, P], BF16)
        x_pad = sb("x_pad", [P, SEQ + TAPS - 1])
        u = [sb(f"u{n}", [P, SEQ]) for n in range(2)]
        z = [sb(f"z{n}", [P, SEQ]) for n in range(2)]
        delta = [sb(f"delta{n}", [P, SEQ]) for n in range(2)]
        du = [sb(f"du{n}", [P, SEQ]) for n in range(2)]
        bc_parts = [sb(f"bc_parts{n}", [P, SEQ], BF16) for n in range(2)]
        y_sb = sb("y_sb", [P, SEQ])

        shared = dict(locals())
        setup = Setup(nc, ctx, shared)
        f1 = moe_phase(nc, ctx, "f1", shared, setup, None, None)
        mamba = mamba_phase(nc, ctx, shared, setup, f1)
        f2 = moe_phase(nc, ctx, "f2", shared, None, out, mamba)
        for phase, following in ((f1, mamba), (mamba, f2), (f2, None)):
            with phase.buffers():
                run_block(nc, phase, following)


class Phase:

    def __init__(self, nc, tag, own, **sems):
        self.nc, self.tag, self.own, self.sems = nc, tag, own, sems
        self.programs, self.started, self.buffer = {}, {}, {}

    def buffers(self):
        room = ExitStack()
        for name, shape, dt in self.own:
            self.buffer[name] = room.enter_context(self.nc.sbuf_tensor(f"{self.tag}_{name}", shape, dt))
        return room

    def stage(self, engine, queue):
        if engine not in self.started:
            self.started[engine] = self.programs[engine](queue)
        next(self.started[engine], None)


def run_block(nc, phase, following):
    def stages(engine, queue):
        if engine not in phase.started:
            phase.stage(engine, queue)
        phase.stage(engine, queue)
        if following:
            following.stage(engine, queue)
        phase.stage(engine, queue)

    with nc.Block() as block:
        @block.sync
        def _(sp):
            stages("sync", sp)

        @block.gpsimd
        def _(pool):
            stages("gpsimd", pool)

        @block.scalar
        def _(ae):
            stages("scalar", ae)

        @block.vector
        def _(dve):
            stages("vector", dve)

        @block.tensor
        def _(pe):
            stages("tensor", pe)


class Setup:

    CHUNKS = [(0, NSH), (NE - LAG, NE), (NSH, 6), (6, 10), (10, NE - LAG)]

    DVE_CHUNKS = 3
    SELECTS = 2 * (1 + PARTS)

    def __init__(self, nc, ctx, m):
        self.nc, self.m = nc, m

        def sem(name):
            return ctx.enter_context(nc.semaphore(name))

        self.x_first, self.x_rest = sem("x_first"), sem("x_rest")
        self.router_loaded, self.small_loaded = sem("router_loaded"), sem("small_loaded")
        self.experts_loaded = [sem(f"experts_loaded{n}") for n in range(len(self.CHUNKS))]
        self.idents, self.halves, self.selects = sem("idents"), sem("halves"), sem("selects")
        self.zeroed, self.consts = sem("zeroed"), sem("consts")
        self.selectors_done, self.edges, self.lo_pool = sem("selectors_done"), sem("edges"), sem("lo_pool")
        self.hi_done, self.lo_done, self.taps_done = sem("hi_done"), sem("lo_done"), sem("taps_done")
        self.xp_pe, self.xp_act, self.a_step = sem("xp_pe"), sem("xp_act"), sem("a_step")

    def load(self, sp):
        m = self.m
        x_sb, stage, x_in = m["x_sb"], m["stage"], m["x_in"]
        sp.dma_start(x_sb[:, 1], x_in[0].rearrange("(t p) d -> p t d", p=P)).then_inc(self.x_first, 16)
        sp.dma_start(m["router_sb"][:, :], m["router_w"]).then_inc(self.router_loaded, 16)
        sp.dma_start(m["bias_sb"][:, :, :],
                     m["route_bias"].partition_broadcast(P).unsqueeze(1).broadcast_to([P, TT, E])
                     ).then_inc(self.router_loaded, 16)
        for (a, b), done in zip(self.CHUNKS, self.experts_loaded):
            if a == 0:
                srcs = (m["sh_gate_w"].rearrange("d (q f) -> d q f", q=NSH),
                        m["sh_up_w"].rearrange("d (q f) -> d q f", q=NSH),
                        m["sh_down_w"].rearrange("(q f) d -> f q d", q=NSH))
            else:
                srcs = [m[n][a - NSH:b - NSH].rearrange("e r c -> r e c") for n in ("gate_w", "up_w", "down_w")]
            for n, src in enumerate(srcs):
                sp.dma_start(stage[:, a:b, n, :], src).then_inc(done, 16)
        sp.dma_start(x_sb[:, 2:BATCH + 1], x_in[1:BATCH].rearrange("b (t p) d -> p b t d", p=P)
                     ).then_inc(self.x_rest, 16)
        small = [(m["w_in_sb"][:, :, :], m["w_in"].rearrange("d (h c) -> d h c", h=2)),
                 (m["taps_row"][:, 0].rearrange("p c k -> p (c k)"), m["k_x"].partition_broadcast(P)),
                 (m["taps_row"][:, 1].rearrange("p c k -> p (c k)"), m["k_z"].partition_broadcast(P)),
                 (m["w_xp"][:, :], m["w_xproj"]), (m["w_dt_sb"][:, :], m["w_dt"]),
                 (m["w_out_sb"][:, :, :], m["w_out"].rearrange("(h c) d -> c h d", h=2)),
                 (m["b_x_sb"][:, :], m["b_x"]), (m["b_z_sb"][:, :], m["b_z"]), (m["b_dt_sb"][:, :], m["b_dt"]),
                 (m["d_sb"][:, :], m["d_skip"]), (m["a_log_sb"][:, :], m["a_log"])]
        for dst, src in small:
            sp.dma_start(dst, src).then_inc(self.small_loaded, 16)
        self.small = 16 * len(small)

    def wait_small(self, eng):
        eng.wait_ge(self.small_loaded, self.small)

    def pool_first(self, pool):
        nc, m = self.nc, self.m
        for v in (m["ident"], m["ident_bf"]):
            nc.gpsimd.memset(v[:], 0.0).then_inc(self.idents, 1)
        nc.gpsimd.memset(m["before"][:], 1.0).then_inc(self.idents, 1)
        nc.gpsimd.memset(m["minus_half"][:], -0.5).then_inc(self.halves, 1)
        pool.wait_ge(self.idents, 3)
        for v in (m["ident"], m["ident_bf"]):
            nc.gpsimd.affine_select(out=v[:], in_=v[:], compare_op=ALU.not_equal, fill=1.0, base=0,
                                    pattern=[[-1, P]], channel_multiplier=1).then_inc(self.idents, 1)
        nc.gpsimd.affine_select(out=m["before"][:], in_=m["before"][:], compare_op=ALU.is_gt, fill=0.0, base=0,
                                pattern=[[1, GROUPS], [-1, GROUPS]], channel_multiplier=0).then_inc(self.idents, 1)
        pool.wait_ge(self.halves, 1)

    def pool_zeros(self, pool):
        nc, m = self.nc, self.m
        for v in (m["act_hi"][:].bitcast(FP32), m["act_lo"][:].bitcast(FP32)):
            nc.gpsimd.memset(v, 0.0).then_inc(self.zeroed, 1)

    def pool_second(self, pool):
        nc, m = self.nc, self.m
        steps = Steps(pool, self.selects, 0)
        for v in (m["sel_e_row"], m["sel_n_row"]):
            steps.do(nc.gpsimd.memset(v[:], 0.0))
        for part in range(PARTS):
            steps.settle()
            for v, rows in ((m["sel_e_row"], E), (m["sel_n_row"], 2 * NS)):
                steps.do(nc.gpsimd.affine_select(out=v[:], in_=v[:], compare_op=ALU.not_equal, fill=1.0,
                                                 base=-part * rows, pattern=[[-1, rows]], channel_multiplier=1))
        steps.settle()
        assert steps.n == self.SELECTS
        for v in (m["x_pad"][:, 0:1], m["x_pad"][:, SEQ + 1:SEQ + TAPS - 1], m["bc_parts"][0][:],
                  m["bc_parts"][1][:], m["u"][1][:], m["z"][1][:], m["y_sb"][:]):
            nc.gpsimd.memset(v, 0.0).then_inc(self.edges, 1)
        for n in range(self.DVE_CHUNKS, len(self.CHUNKS)):
            self.low_part(nc.gpsimd, pool, n, self.lo_pool)
        self.wait_small(pool)
        for h in range(2):
            for k in range(TAPS):
                nc.gpsimd.tensor_tensor(m["w_tap"][:, h, k, :], m["w_in_sb"][:, h, :], m["taps_row"][:, h, :, k],
                                        ALU.mult).then_inc(self.taps_done, 1)

    def act_high_parts(self, ae, chunks):
        for n in chunks:
            a, b = self.CHUNKS[n]
            ae.wait_ge(self.experts_loaded[n], 48)
            self.nc.scalar.activation(self.m["w_hi"][:, a:b], self.m["stage"][:, a:b], ACT.Copy
                                      ).then_inc(self.hi_done, 1)

    def act_selector(self, ae, name, rows):
        m = self.m
        ae.wait_ge(self.selects, self.SELECTS)
        self.nc.scalar.activation(m[name][:], m[f"{name}_row"][:].unsqueeze(2).broadcast_to([P, rows, P]),
                                  ACT.Copy).then_inc(self.selectors_done, 1)

    def low_part(self, engine, queue, n, done):
        a, b = self.CHUNKS[n]
        flat = lambda v: v[:, a:b].rearrange("p e n c -> p (e n c)")
        queue.wait_ge(self.hi_done, n + 1)
        engine.tensor_tensor(flat(self.m["w_lo"]), flat(self.m["stage"]),
                             flat(self.m["w_hi"]).bitcast(FP32), ALU.subtract).then_inc(done, 1)

    def dve_low_parts(self, dve, chunks):
        for n in chunks:
            self.low_part(self.nc.vector, dve, n, self.lo_done)

    def pe_wait_parts(self, pe, k):
        for n, (a, _) in enumerate(self.CHUNKS):
            if n == 1:
                a = 0
            if k == a and n < self.DVE_CHUNKS:
                pe.wait_ge(self.lo_done, n + 1)
            elif k == a:
                pe.wait_ge(self.lo_pool, n + 1 - self.DVE_CHUNKS)

    def dve_zeros(self, dve):
        nc, m = self.nc, self.m
        zero = Steps(dve, self.consts, 0)
        for v in (m["x_sb"][:, 0], m["x_sb"][:, BATCH + 1:], m["c_parts"][:]):
            zero.do(nc.vector.memset(v, 0.0))
        zero.do(nc.vector.memset(m["same_tile"][:], 1.0))
        for n, (a, b) in enumerate(LOG1P):
            if n == len(LOG1P) - 1:
                b *= LOG1P_SCALE
            zero.do(nc.vector.memset(m["log_consts"][:, 2 * n:2 * n + 1], a))
            zero.do(nc.vector.memset(m["log_consts"][:, 2 * n + 1:2 * n + 2], b))
        zero.settle()
        zero.do(nc.vector.memset(m["same_tile"][:, :, 0:1], 0.0))
        zero.settle()

    def pe_delta_weight(self, pe, bank):
        nc, m = self.nc, self.m
        self.wait_small(pe)
        nc.tensor.transpose(bank[0:RANK, 0, 0:P], m["w_xp"][:, 0:RANK], m["ident"][:, :]).then_inc(self.xp_pe, 1)
        pe.wait_ge(self.xp_act, 1)
        nc.tensor.matmul(bank[:, 1, 0:P], m["w_xp_t"][:, :], m["w_dt_sb"][:, :], start=True,
                         stop=True).then_inc(self.xp_pe, 1)

    def act_delta_weight(self, ae, bank):
        nc, m = self.nc, self.m
        ae.wait_ge(self.xp_pe, 1)
        nc.scalar.activation(m["w_xp_t"][:, :], bank[0:RANK, 0, 0:P], ACT.Copy).then_inc(self.xp_act, 1)
        ae.wait_ge(self.xp_pe, 2)
        nc.scalar.activation(m["w_delta"][:, :], bank[:, 1, 0:P], ACT.Copy).then_inc(self.xp_act, 1)

    def act_decay_rates(self, ae):
        nc, m = self.nc, self.m
        nc.scalar.activation(m["a_neg"][:, :], m["a_log_sb"][:, :], ACT.Exp).then_inc(self.a_step, 1)
        ae.wait_ge(self.a_step, 1)
        nc.scalar.mul(m["a_neg"][:, :], m["a_neg"][:, :], -1.0).then_inc(self.a_step, 1)
        ae.wait_ge(self.a_step, 2)


def norm_stats(nc, steps, x_sb, slot, stats, mean_var, var_eps, ready):
    for t in range(TT):
        steps.do(nc.vector.bn_stats(stats[:, t, :], x_sb[:, slot, t, :]))
    yield
    steps.settle_apart()
    for t in range(TT):
        steps.do(nc.vector.bn_aggr(mean_var[:, t, :], stats[:, t, :]))
    steps.settle()
    nc.vector.tensor_scalar(var_eps[:, :], mean_var[:, :, 1], EPS, None, ALU.add).then_inc(ready, 1)
    yield


def norm_apply(nc, x_sb, slot, xn, mean_var, rstd, done):
    for t in range(TT):
        nc.vector.tensor_scalar(xn[:, t, :], x_sb[:, slot, t, :], mean_var[:, t, 0:1], rstd[:, t:t + 1],
                                ALU.subtract, ALU.mult).then_inc(done, 1)


def moe_phase(nc, ctx, tag, m, setup, out, before_it):
    (x_sb, ident, ident_bf, w_hi, w_lo, xn, stats, mean_var, var_eps, rstd, minus_half, bank, router_sb,
     bias_sb, sel_e, before, same_tile, xt, sg, act, act_hi, act_lo, out_t, c_t, c_parts, th,
     score, biased, pair_sum, g_score, g_ge, g_gt, g_rank, g_in, masked, top8, above, tied, n_above, tie_at,
     picked, total, comb, rest) = (m[n] for n in (
         "x_sb ident ident_bf w_hi w_lo xn stats mean_var var_eps rstd minus_half bank router_sb bias_sb "
         "sel_e before same_tile xt sg act act_hi act_lo out_t c_t c_parts th score biased "
         "pair_sum g_score g_ge g_gt g_rank g_in masked top8 above tied n_above tie_at picked total comb "
         "rest").split())
    h_bank, u_bank, c_bank = (bank[n] for n in range(3))
    acc, misc = bank[3][:, 0, :], bank[3][:, 1, :]
    misc_bf = misc.bitcast(BF16)

    def sem(name):
        return ctx.enter_context(nc.semaphore(f"{tag}_{name}"))

    h_ready, u_ready, cb_ready = sem("h_ready"), sem("u_ready"), sem("cb_ready")
    sg_ready = sem("sg_ready")
    w_done = sem("w_done")
    act_ready = sem("act_ready")
    hi_ready = sem("hi_ready")
    lo_ready = sem("lo_ready")
    down_done = sem("down_done")
    acc_read, ot_ready, x_added = sem("acc_read"), sem("ot_ready"), sem("x_added")
    var_ready, rstd_ready, xn_ready = sem("var_ready"), sem("rstd_ready"), sem("xn_ready")
    xt_ready, xt_copied, logits_ready, tanh_ready = (
        sem("xt_ready"), sem("xt_copied"), sem("logits_ready"), sem("tanh_ready"))
    parts_ready, ct_ready, ct_copied, x_split = (
        sem("parts_ready"), sem("ct_ready"), sem("ct_copied"), sem("x_split"))
    norm_step, route_step, stored = sem("norm_step"), sem("route_step"), sem("stored")
    ROUTE_STEPS = 34

    phase = Phase(nc, tag, [("x_hi", [P, 2, SEQ], F32R), ("x_lo", [P, 2, SEQ], F32R)], w_done=w_done)

    def sync_program(sp):
        if setup:
            setup.load(sp)
        yield
        if out is not None:
            rows = out.rearrange("b (t p) d -> b p t d", p=P)
            with sp.Fori(0, BATCH) as i:
                sp.wait_ge(x_added, i + 2)
                sp.dma_start(rows[i], x_sb[:, i + 1]).then_inc(stored, 16)
            sp.wait_ge(stored, 16 * BATCH)
        yield

    def gpsimd_program(pool):
        def norm_root(r):
            pool.wait_ge(var_ready, r + 1)
            nc.gpsimd.tensor_tensor(rstd[:, :], var_eps[:, :], minus_half[:, :], ALU.pow).then_inc(rstd_ready, 1)

        if setup:
            setup.pool_first(pool)
            setup.pool_zeros(pool)
        norm_root(0)
        yield
        if setup:
            setup.pool_second(pool)
        with pool.Fori(0, BATCH // 2) as turn:
            for q in range(2):
                i = turn * 2 + q
                for k in range(NE):
                    if k == 3:
                        norm_root(i + 1)
                    g = i * NE + k
                    pool.wait_ge(hi_ready, g + 1)
                    nc.gpsimd.tensor_tensor(act_lo[:, k % 3], act[:, k % 2], act_hi[:, k % 3].bitcast(FP32),
                                            ALU.subtract).then_inc(lo_ready, 1)
        yield

    def scalar_program(ae):
        nc.scalar.preload_act_table_set("silu_and_others")

        def copy_xt(r):
            ae.wait_ge(xt_ready, r + 1)
            nc.scalar.activation(xt[:, :], misc, ACT.Copy).then_inc(xt_copied, 1)

        def tanh(r):
            ae.wait_ge(logits_ready, r + 1)
            nc.scalar.activation(th[:].rearrange("p t e -> p (t e)"), misc[:, 0:TT * E], ACT.Tanh,
                                 scale=0.5).then_inc(tanh_ready, 1)

        def read_acc(i):
            nc.scalar.activation(out_t[:, :], acc, ACT.Copy, scale=0.5).then_inc(acc_read, 1)

        copy_xt(0)
        if setup:
            setup.act_high_parts(ae, [0])
        tanh(0)
        yield
        if setup:
            setup.act_high_parts(ae, [1])
            setup.act_selector(ae, "sel_e", E)
            setup.act_high_parts(ae, [2, 3, 4])
            setup.act_selector(ae, "sel_n", 2 * NS)
        with ae.Fori(0, BATCH // 2) as turn:
            for q in range(2):
                i = turn * 2 + q
                for k in range(NE):
                    g = i * NE + k
                    if k == 1:
                        ae.wait_ge(ct_ready, i + 1)
                        nc.scalar.activation(c_t[:, :], misc_bf[:, 0:SEQ], ACT.Copy).then_inc(ct_copied, 1)
                    ae.wait_ge(h_ready, g + 1)
                    ae.wait_ge(act_ready, g + 1)
                    nc.scalar.activation(sg[:, k % 2], h_bank[:, k % 2], ACT.Silu).then_inc(sg_ready, 1)
                    for j in ([k - 1] if k else []) + ([k] if k == NE - 1 else []):
                        ae.wait_ge(act_ready, i * NE + j + 3)
                        ae.wait_ge(down_done, i * NE + j + LAG - 1)
                        nc.scalar.activation(act_hi[:, j % 3], act[:, j % 2], ACT.Copy).then_inc(hi_ready, 1)
                    if k == LAG - 1:
                        ae.wait_ge(down_done, i * NE + LAG + 1)
                        read_acc(i)
                    if k == 6:
                        ae.wait_ge(x_split, 2 * i + 2)
                        copy_xt(i + 1)
                    if k == 8:
                        tanh(i + 1)
        if setup:
            setup.act_delta_weight(ae, c_bank)
        yield
        ae.wait_ge(down_done, BATCH * NE + LAG + 1)
        ae.wait_ge(ot_ready, BATCH)
        read_acc(BATCH)

    def vector_program(dve):
        x_hi, x_lo = (phase.buffer.get(name) for name in ("x_hi", "x_lo"))
        dve.sem_inc(sg_ready, 2)
        dve.sem_inc(w_done, 2)
        dve.sem_inc(act_ready, 2)
        dve.sem_inc(lo_ready, LAG)
        dve.sem_inc(down_done, 1)

        def stats_of(r, slot):
            steps = Steps(dve, norm_step, r * LN_STEPS)
            return norm_stats(nc, steps, x_sb, slot, stats, mean_var, var_eps, var_ready)

        def apply_to(r, slot):
            dve.wait_ge(rstd_ready, r + 1)
            norm_apply(nc, x_sb, slot, xn, mean_var, rstd, xn_ready)

        def route(r, first=False):
            s = Steps(dve, route_step, r * ROUTE_STEPS)
            flat = lambda a: a[:].rearrange("p t e -> p (t e)")
            grouped = lambda a: a[:].rearrange("p t (g e) -> p (t g) e", g=GROUPS)
            gs = g_score[:].rearrange("p t g -> p (t g)")
            dve.wait_ge(tanh_ready, r + 1)
            s.do(nc.vector.tensor_scalar(flat(score), flat(th), 0.5, 0.5, ALU.mult, ALU.add))
            s.settle()
            s.do(nc.vector.tensor_tensor(flat(biased), flat(score), flat(bias_sb), ALU.add))
            s.settle()
            yield
            b4, at = grouped(biased), 0
            for gap in range(1, EPG):
                n = EPG - gap
                s.do(nc.vector.tensor_tensor(pair_sum[:, :, at:at + n], b4[:, :, 0:n], b4[:, :, gap:EPG],
                                             ALU.add))
                at += n
            s.settle()
            s.do(nc.vector.tensor_reduce(gs, pair_sum[:], AX.X, ALU.max))
            s.settle()
            yield
            other = g_score[:].unsqueeze(2).broadcast_to([P, TT, GROUPS, GROUPS])
            own = g_score[:].unsqueeze(3).broadcast_to([P, TT, GROUPS, GROUPS])
            s.do(nc.vector.tensor_tensor(g_ge[:], other, own, ALU.is_ge))
            s.do(nc.vector.tensor_tensor(g_gt[:], other, own, ALU.is_gt))
            s.settle()
            s.do(nc.vector.tensor_tensor(g_ge[:], g_ge[:],
                                         before[:].unsqueeze(1).broadcast_to([P, TT, GROUPS, GROUPS]),
                                         ALU.mult))
            s.settle()
            s.do(nc.vector.tensor_tensor(g_ge[:], g_ge[:], g_gt[:], ALU.max))
            s.settle()
            s.do(nc.vector.tensor_reduce(g_rank[:], g_ge[:].rearrange("p t g h -> p (t g) h"), AX.X, ALU.add))
            s.settle()
            yield
            s.do(nc.vector.tensor_scalar(g_in[:], g_rank[:], float(TOP_GROUPS), None, ALU.is_lt))
            s.settle()
            g_in_e = g_in[:].unsqueeze(2).broadcast_to([P, TT * GROUPS, EPG])
            s.do(nc.vector.tensor_tensor(grouped(masked), grouped(biased), g_in_e, ALU.mult))
            s.settle()
            s.do(nc.vector.scalar_tensor_tensor(grouped(masked), g_in_e, -1.0, grouped(masked),
                                                ALU.add, ALU.add))
            yield
            s.settle_apart()
            for t in range(TT):
                s.do(nc.vector.max(top8[:, t, :], masked[:, t, :]))
            s.settle()
            yield
            fourth = top8[:, :, TOP_EXPERTS - 1:TOP_EXPERTS].broadcast_to([P, TT, E])
            s.do(nc.vector.tensor_tensor(above[:], masked[:], fourth, ALU.is_gt))
            s.do(nc.vector.tensor_tensor(tied[:], masked[:], fourth, ALU.is_equal))
            s.settle()
            s.do(nc.vector.tensor_reduce(n_above[:], above[:], AX.X, ALU.add))
            s.do(nc.vector.tensor_tensor_scan(flat(tie_at), flat(same_tile), flat(tied), 0.0,
                                              ALU.mult, ALU.add))
            s.settle()
            s.do(nc.vector.tensor_tensor(tie_at[:], tie_at[:],
                                         n_above[:].unsqueeze(2).broadcast_to([P, TT, E]), ALU.add))
            s.settle()
            s.do(nc.vector.scalar_tensor_tensor(flat(picked), flat(tie_at), float(TOP_EXPERTS), flat(tied),
                                                ALU.is_le, ALU.mult))
            s.settle()
            yield
            s.do(nc.vector.tensor_tensor(picked[:], picked[:], above[:], ALU.add))
            s.settle()
            s.do(nc.vector.tensor_tensor(picked[:], picked[:], score[:], ALU.mult))
            s.settle()
            s.do(nc.vector.tensor_reduce(total[:], picked[:], AX.X, ALU.add))
            s.settle()
            yield
            s.do(nc.vector.tensor_scalar(total[:], total[:], 1e-20, None, ALU.add))
            s.settle()
            s.do(nc.vector.reciprocal(total[:], total[:]))
            s.settle()
            s.do(nc.vector.scalar_tensor_tensor(comb[:], picked[:], ROUTE_SCALE,
                                                total[:].unsqueeze(2).broadcast_to([P, TT, E]),
                                                ALU.mult, ALU.mult))
            s.settle()
            yield
            if not first:
                dve.wait_ge(ct_ready, r)
            s.do(nc.vector.tensor_copy(c_parts[:, :, 0:E], comb[:]))
            s.settle()
            s.do(nc.vector.tensor_tensor(rest[:], comb[:], c_parts[:, :, 0:E], ALU.subtract))
            s.settle()
            s.do(nc.vector.tensor_copy(c_parts[:, :, E:2 * E], rest[:]))
            s.settle()
            nc.vector.tensor_tensor(c_parts[:, :, 2 * E:3 * E], rest[:], c_parts[:, :, E:2 * E],
                                    ALU.subtract).then_inc(parts_ready, 1)
            assert s.n == ROUTE_STEPS, s.n
            yield

        def split_x(r, q):
            dve.wait_ge(xt_copied, r + 1)
            nc.vector.tensor_copy(x_hi[:, q], xt[:, :]).then_inc(x_split, 1)
            yield
            dve.wait_ge(x_split, 2 * r + 1)
            nc.vector.tensor_tensor(x_lo[:, q], xt[:, :], x_hi[:, q].bitcast(FP32),
                                    ALU.subtract).then_inc(x_split, 1)
            yield

        def add_rows(i):
            dve.wait_ge(ot_ready, i + 1)
            nc.vector.tensor_tensor(x_sb[:, i], x_sb[:, i], misc.rearrange("p (t d) -> p t d", t=TT),
                                    ALU.add).then_inc(x_added, 1)

        if setup:
            dve.wait_ge(setup.x_first, 16)
        run(stats_of(0, 1))
        if before_it:
            dve.wait_ge(before_it.sems["xt_ready"], BATCH + 2)
        apply_to(0, 1)
        if setup:
            setup.dve_zeros(dve)
            dve.wait_ge(setup.router_loaded, 32)
            dve.wait_ge(setup.idents, 6)
        if setup:
            run(split_x(0, 0))
            setup.dve_low_parts(dve, [0])
            run(route(0, first=True))
        yield
        if not setup:
            x_hi, x_lo = (phase.buffer[name] for name in ("x_hi", "x_lo"))
            run(split_x(0, 0))
            run(route(0, first=True))
        if setup:
            setup.dve_low_parts(dve, range(1, setup.DVE_CHUNKS))
            dve.wait_ge(setup.x_rest, 16)
        with dve.Fori(0, BATCH // 2) as turn:
            for q in range(2):
                i = turn * 2 + q
                norming, routing, splitting = stats_of(i + 1, i + 2), route(i + 1), split_x(i + 1, 1 - q)
                for k in range(NE):
                    g = i * NE + k
                    dve.wait_ge(sg_ready, g + 3)
                    if k >= NSH:
                        r = i * E + (k - NSH)
                        dve.wait_ge(cb_ready, r + 1)
                        nc.vector.tensor_tensor(sg[:, k % 2], sg[:, k % 2], c_bank[:, k % 2],
                                                ALU.mult).then_inc(w_done, 1)
                    dve.wait_ge(u_ready, g + 1)
                    if k >= NSH:
                        dve.wait_ge(w_done, r + 3)
                    dve.wait_ge(lo_ready, g + LAG - 1)
                    nc.vector.tensor_tensor(act[:, k % 2], sg[:, k % 2], u_bank[:, k % 2],
                                            ALU.mult).then_inc(act_ready, 1)
                    if k in (1, 2):
                        next(norming)
                    if k == 4:
                        dve.wait_ge(xt_ready, i + 1)
                        apply_to(i + 1, i + 2)
                    if k == 5:
                        add_rows(i)
                    if k in (7, 8):
                        next(splitting)
                    if k == 9:
                        next(routing)
                    if 9 <= k <= 16:
                        next(routing)
        yield
        add_rows(BATCH)
        dve.wait_ge(x_added, BATCH + 1)

    def tensor_program(pe):
        def transpose_xn(r):
            pe.wait_ge(xn_ready, TT * (r + 1))
            for t in range(TT):
                last = nc.tensor.transpose(misc[:, t * P:(t + 1) * P], xn[:, t, :], ident[:, :])
            last.then_inc(xt_ready, 1)

        def logits(r):
            pe.wait_ge(xt_copied, r + 1)
            for t in range(TT):
                last = nc.tensor.matmul(misc[:, t * E:(t + 1) * E], xt[:, t * P:(t + 1) * P],
                                        router_sb[:, :], start=True, stop=True)
            last.then_inc(logits_ready, 1)

        def transpose_parts(r):
            pe.wait_ge(tanh_ready, r + 1)
            pe.wait_ge(parts_ready, r + 1)
            for t in range(TT):
                last = nc.tensor.transpose(misc_bf[:, t * P:(t + 1) * P], c_parts[:, t, :], ident_bf[:, :])
            last.then_inc(ct_ready, 1)

        def down(i, k):
            j = k % NE
            pe.wait_ge(lo_ready, i * NE + k + 1 + LAG)
            if k == 0:
                pe.wait_ge(acc_read, i + 1)
            dt = w_hi[:, j, 2, :], w_lo[:, j, 2, :]
            first, last = j == 0, j == NE - 1
            nc.tensor.matmul(acc, dt[0], act_hi[:, j % 3], start=first, stop=False, skip_group_check=True)
            nc.tensor.matmul(acc, dt[1], act_hi[:, j % 3], start=False, stop=False, skip_group_check=True)
            nc.tensor.matmul(acc, dt[0], act_lo[:, j % 3], start=False, stop=last,
                             skip_group_check=True).then_inc(down_done, 1)

        def transpose_out(i):
            pe.wait_ge(acc_read, i + 1)
            for t in range(TT):
                last = nc.tensor.transpose(misc[:, t * P:(t + 1) * P], out_t[:, t * P:(t + 1) * P], ident[:, :])
            last.then_inc(ot_ready, 1)

        def product(dst, n, k, q, new_row=None):
            if new_row is not None:
                pe.wait_ge(x_split, 2 * new_row + 1)
            nc.tensor.matmul(dst, w_hi[:, k, n, :], x_hi[:, q], start=True, stop=False)
            nc.tensor.matmul(dst, w_lo[:, k, n, :], x_hi[:, q], start=False, stop=False)
            if new_row is not None:
                pe.wait_ge(x_split, 2 * new_row + 2)
            return nc.tensor.matmul(dst, w_hi[:, k, n, :], x_lo[:, q], start=False, stop=True)

        if setup:
            pe.wait_ge(setup.idents, 6)
        else:
            pe.wait_ge(before_it.sems["gated"], 2 * (BATCH + 1))
        transpose_xn(0)
        if setup:
            pe.wait_ge(setup.router_loaded, 32)
        logits(0)
        yield
        x_hi, x_lo = (phase.buffer[name] for name in ("x_hi", "x_lo"))
        if setup:
            pe.wait_ge(setup.zeroed, 2)
            pe.wait_ge(setup.hi_done, 1)
            pe.wait_ge(setup.selectors_done, 1)
        nc.tensor.matmul(acc, w_hi[:, 0, 2, :], act_hi[:, 1], start=True, stop=True)
        with pe.Fori(0, BATCH // 2) as turn:
            for q in range(2):
                i = turn * 2 + q
                for k in range(NE):
                    g = i * NE + k
                    if setup:
                        setup.pe_wait_parts(pe, k)
                    pe.wait_ge(sg_ready, g + 1)
                    product(h_bank[:, k % 2], 0, k, q, i if k == 0 else None).then_inc(h_ready, 1)
                    if k < LAG:
                        down(i, k - LAG)
                    pe.wait_ge(act_ready, g + 1)
                    product(u_bank[:, k % 2], 1, k, q).then_inc(u_ready, 1)
                    if k == 0:
                        transpose_parts(i)
                    if k >= NSH:
                        r = i * E + (k - NSH)
                        pe.wait_ge(ct_copied, i + 1)
                        pe.wait_ge(w_done, r + 1)
                        nc.tensor.matmul(c_bank[:, k % 2], sel_e[:, k - NSH, :], c_t[:, :], start=True,
                                         stop=True).then_inc(cb_ready, 1)
                    if k >= LAG:
                        down(i, k - LAG)
                    if k == 4:
                        pe.wait_ge(ct_copied, i + 1)
                        transpose_out(i)
                    if k == 6:
                        pe.wait_ge(x_added, i + 1)
                        transpose_xn(i + 1)
                    if k == 8:
                        logits(i + 1)
        if setup:
            pe.wait_ge(w_done, BATCH * E + 2)
            setup.pe_delta_weight(pe, c_bank)
        for k in range(-LAG, 0):
            down(BATCH, k)
        yield
        transpose_out(BATCH)

    phase.programs = dict(sync=sync_program, gpsimd=gpsimd_program, scalar=scalar_program,
                          vector=vector_program, tensor=tensor_program)
    return phase


def mamba_phase(nc, ctx, m, setup, before_it):
    (x_sb, ident, xn, stats, mean_var, var_eps, rstd, minus_half, bank, w_tap, w_xp, w_delta, w_out_sb,
     b_x_sb, b_z_sb, b_dt_sb, d_sb, a_neg, log_consts, sel_n, x_pad, u, z, delta, du, bc_parts, y_sb, stage) = (
        m[n] for n in (
            "x_sb ident xn stats mean_var var_eps rstd minus_half bank w_tap w_xp w_delta w_out_sb b_x_sb "
            "b_z_sb b_dt_sb d_sb a_neg log_consts sel_n x_pad u z delta du bc_parts y_sb stage").split())
    b_bank, c_bank = bank[0], bank[1]
    y_acc, misc = bank[2][:, 0, :], bank[2][:, 1, :]
    front = bank[3]

    room = stage[:].rearrange("p a b c -> p (a b c)")
    at = [0]

    def place(*shape):
        n = int(np.prod(shape))
        at[0] += n
        v = room[:, at[0] - n:at[0]]
        return v.rearrange("p (a s l) -> p a s l", a=shape[0], s=shape[1]) if len(shape) == 3 else (
            v.rearrange("p (s l) -> p s l", s=shape[0]) if len(shape) == 2 else v)

    decay = place(2, 2, SEQ)
    state_in = place(2, SEQ), m["taps_row"][:].rearrange("p h c k -> p (h c k)").rearrange(
        "p (s l) -> p s l", s=2)
    state_c = place(2, 2, SEQ)
    soft_abs, soft_relu, soft_e = m["sg"][:, 0], m["sg"][:, 1], m["act"][:, 0]
    soft_factors = soft_abs, m["act"][:, 1], m["out_t"][:, :], place(SEQ)
    rest, second = m["xt"][:, :], m["c_t"][:, :]
    assert at[0] <= NE * 3 * P

    def sem(name):
        return ctx.enter_context(nc.semaphore(f"mb_{name}"))

    var_ready, rstd_ready, xn_ready, norm_step = (
        sem("var_ready"), sem("rstd_ready"), sem("xn_ready"), sem("norm_step"))
    xt_ready, xt_copied, conv_ready, gated = sem("xt_ready"), sem("xt_copied"), sem("conv_ready"), sem("gated")
    bc_ready, dt_ready = sem("bc_ready"), sem("dt_ready")
    first_part, rest_ready, second_part, parts_ready = (
        sem("first_part"), sem("rest_ready"), sem("second_part"), sem("parts_ready"))
    soft_act, soft_pool, du_ready = sem("soft_act"), sem("soft_pool"), sem("du_ready")
    b_ready, c_ready, decay_ready = sem("b_ready"), sem("c_ready"), sem("decay_ready")
    in_done = sem("in_done")
    scan_done = sem("scan_done")
    mul_done = sem("mul_done")
    sum_done = sem("sum_done")
    out_ready = sem("out_ready")
    x_added = sem("x_added")
    y_ready, zeroed = sem("y_ready"), sem("zeroed")
    pair_added = sem("pair_added")
    ACT_SOFT, POOL_SOFT = 11, 5
    SQUARES = 7
    SOFT_PIECES = (0, 0, 0, 1, 2, 2, 1, 0)

    phase = Phase(nc, "mb", [("states", [P, 2, 2, SEQ], FP32)], gated=gated, xt_ready=xt_ready)

    def sync_program(sp):
        yield
        yield

    def gpsimd_program(pool):
        def norm_root(r):
            pool.wait_ge(var_ready, r + 1)
            nc.gpsimd.tensor_tensor(rstd[:, :], var_eps[:, :], minus_half[:, :], ALU.pow).then_inc(rstd_ready, 1)

        def soft(r, q):
            count = Steps(pool, soft_pool, r * POOL_SOFT)
            pool.wait_ge(soft_act, (r + 1) * ACT_SOFT)
            product = soft_e
            for factor in soft_factors:
                count.settle()
                count.do(nc.gpsimd.tensor_tensor(soft_e, product, factor, ALU.mult))
                yield
            count.settle()
            count.do(nc.gpsimd.tensor_tensor(delta[q][:, :], soft_e, soft_relu, ALU.add))
            assert count.n == POOL_SOFT
            yield
            count.settle()
            nc.gpsimd.tensor_tensor(du[q][:, :], delta[q][:, :], u[q][:, :], ALU.mult).then_inc(du_ready, 1)
            yield

        norm_root(0)
        yield
        norm_root(1)
        with pool.Fori(0, BATCH // 2) as turn:
            for q in range(2):
                i = turn * 2 + q
                softening = soft(i + 1, 1 - q)
                for n in range(PAIRS):
                    pool.wait_ge(mul_done, i * PAIRS + n + 3)
                    both = state_c[:, n % 2]
                    nc.gpsimd.tensor_tensor(both[:, 0], both[:, 0], both[:, 1], ALU.add).then_inc(pair_added, 1)
                    if n == 3:
                        norm_root(i + 2)
                    for _ in range(SOFT_PIECES[n]):
                        next(softening)
        yield

    def scalar_program(ae):
        def copy_xt(r):
            ae.wait_ge(xt_ready, r + 1)
            nc.scalar.activation(x_pad[:, 1:SEQ + 1], misc, ACT.Copy).then_inc(xt_copied, 1)

        def gelu(r, h, dst, bias):
            ae.wait_ge(conv_ready, 2 * r + 1 + h)
            nc.scalar.activation(dst[:, :], front[:, h, :], ACT.Gelu, bias=bias[:, 0:1]).then_inc(gated, 1)
            nc.scalar.preload_act_table_set("exp_and_others")

        def parts(r, q):
            ae.wait_ge(bc_ready, r + 1)
            nc.scalar.activation(bc_parts[q][0:2 * NS, :], front[0:2 * NS, 0, :], ACT.Copy).then_inc(first_part, 1)
            yield
            ae.wait_ge(rest_ready, r + 1)
            nc.scalar.activation(second[0:2 * NS, :], rest[0:2 * NS, :], ACT.Copy).then_inc(second_part, 1)
            yield
            nc.scalar.activation(bc_parts[q][2 * NS:4 * NS, :], rest[0:2 * NS, :], ACT.Copy).then_inc(parts_ready, 1)
            yield

        def soft(r):
            s = Steps(ae, soft_act, r * ACT_SOFT)
            ae.wait_ge(dt_ready, r + 1)
            s.do(nc.scalar.activation(soft_abs, front[:, 1, :], ACT.Abs, bias=b_dt_sb[:, 0:1]))
            s.do(nc.scalar.activation(soft_relu, front[:, 1, :], ACT.Relu, bias=b_dt_sb[:, 0:1]))
            s.settle()
            s.do(nc.scalar.activation(soft_e, soft_abs, ACT.Exp, scale=-1.0))
            s.settle()
            yield
            for n, factor in enumerate(soft_factors):
                s.do(nc.scalar.activation(factor, soft_e, ACT.Square, bias=log_consts[:, 2 * n:2 * n + 1]))
            s.settle()
            yield
            for n, factor in enumerate(soft_factors):
                scale = LOG1P_SCALE if n == len(soft_factors) - 1 else 1.0
                s.do(nc.scalar.activation(factor, factor, ACT.Identity, scale=scale,
                                          bias=log_consts[:, 2 * n + 1:2 * n + 2]))
            assert s.n == ACT_SOFT
            yield

        def decays(i, n, q):
            ae.wait_ge(scan_done, i * PAIRS + n + 1)
            if n == 0:
                ae.wait_ge(soft_pool, (i + 1) * POOL_SOFT)
            for s in range(2):
                nc.scalar.activation(decay[:, n % 2, s, 1:SEQ], delta[q][:, 1:SEQ], ACT.Exp,
                                     scale=a_neg[:, 2 * n + s:2 * n + s + 1]).then_inc(decay_ready, 1)

        setup.act_decay_rates(ae)
        copy_xt(0)
        yield
        gelu(0, 0, u[0], b_x_sb)
        softening, splitting = soft(0), parts(0, 0)
        next(softening)
        next(splitting)
        next(softening)
        ae.sem_inc(soft_act, ACT_SOFT - SQUARES)
        run(splitting)
        ae.wait_ge(zeroed, 3)
        decays(0, 0, 0)
        gelu(0, 1, z[0], b_z_sb)
        copy_xt(1)
        with ae.Fori(0, BATCH // 2) as turn:
            for q in range(2):
                i = turn * 2 + q
                for n in range(PAIRS):
                    if n < PAIRS - 1:
                        decays(i, n + 1, q)
                    else:
                        decays(i + 1, 0, 1 - q)
                    if n == 1:
                        ae.wait_ge(y_ready, i + 1)
                        gelu(i + 1, 0, u[1 - q], b_x_sb)
                    if n == 2:
                        ae.wait_ge(soft_pool, (i + 1) * POOL_SOFT)
                        softening, splitting = soft(i + 1), parts(i + 1, 1 - q)
                    if n in (2, 3):
                        next(softening)
                    if n == 3:
                        next(softening)
                    if n in (3, 4, 5):
                        next(splitting)
                    if n == 7:
                        ae.wait_ge(out_ready, i + 2)
                        gelu(i + 1, 1, z[1 - q], b_z_sb)
                        copy_xt(i + 2)
        yield

    def vector_program(dve):
        def stats_of(r, slot):
            steps = Steps(dve, norm_step, r * LN_STEPS)
            return norm_stats(nc, steps, x_sb, slot, stats, mean_var, var_eps, var_ready)

        def apply_to(r, slot):
            dve.wait_ge(rstd_ready, r + 1)
            norm_apply(nc, x_sb, slot, xn, mean_var, rstd, xn_ready)

        def parts(r, q):
            dve.wait_ge(first_part, r + 1)
            nc.vector.tensor_tensor(rest[0:2 * NS, :], front[0:2 * NS, 0, :], bc_parts[q][0:2 * NS, :],
                                    ALU.subtract).then_inc(rest_ready, 1)
            yield
            dve.wait_ge(second_part, r + 1)
            nc.vector.tensor_tensor(bc_parts[q][4 * NS:6 * NS, :], rest[0:2 * NS, :], second[0:2 * NS, :],
                                    ALU.subtract).then_inc(parts_ready, 1)
            yield

        def first_soft():
            count = Steps(dve, soft_pool, 0)
            dve.wait_ge(soft_act, SQUARES)
            for (_, b), square in zip(LOG1P, soft_factors):
                count.settle()
                count.do(nc.vector.scalar_tensor_tensor(soft_e, square, b, soft_e, ALU.add, ALU.mult))
            count.settle()
            count.do(nc.vector.scalar_tensor_tensor(delta[0][:, :], soft_e, LOG1P_SCALE, soft_relu,
                                                    ALU.mult, ALU.add))
            assert count.n == POOL_SOFT
            count.settle()
            nc.vector.tensor_tensor(du[0][:, :], delta[0][:, :], u[0][:, :], ALU.mult).then_inc(du_ready, 1)

        dve.sem_inc(scan_done, 2)
        dve.sem_inc(mul_done, 2)
        for credited in (sum_done, pair_added, out_ready, x_added):
            dve.sem_inc(credited, 1)
        for v in (decay[:, 0, :, 0:1], decay[:, 1, :, 0:1], state_c[:, 1, 0]):
            nc.vector.memset(v, 0.0).then_inc(zeroed, 1)
        run(stats_of(0, 1))
        apply_to(0, 1)
        yield
        states = phase.buffer["states"]
        run(stats_of(1, 2))
        dve.wait_ge(xt_ready, 1)
        apply_to(1, 2)
        splitting = parts(0, 0)
        next(splitting)
        first_soft()
        next(splitting)

        def input_of(g, n, q):
            dve.wait_ge(b_ready, g + 1)
            dve.wait_ge(scan_done, g + 1)
            nc.vector.tensor_tensor(state_in[n % 2], du[q][:, :].unsqueeze(1).broadcast_to([P, 2, SEQ]),
                                    b_bank[:], ALU.mult).then_inc(in_done, 1)

        def finish_y(i, q):
            dve.wait_ge(sum_done, i * PAIRS + 2)
            dve.wait_ge(out_ready, i + 1)
            nc.vector.scalar_tensor_tensor(y_sb[:, :], u[q][:, :], d_sb[:, 0:1], y_acc,
                                           ALU.mult, ALU.add).then_inc(y_ready, 1)

        dve.wait_ge(du_ready, 1)
        input_of(0, 0, 0)
        with dve.Fori(0, BATCH // 2) as turn:
            for q in range(2):
                i = turn * 2 + q
                splitting = parts(i + 1, 1 - q)
                for n in range(PAIRS):
                    g = i * PAIRS + n
                    dve.wait_ge(decay_ready, 2 * g + 2)
                    dve.wait_ge(in_done, g + 1)
                    dve.wait_ge(mul_done, g + 1)
                    nc.vector.tensor_tensor_scan(
                        states[:, n % 2].rearrange("p s l -> p (s l)"),
                        decay[:, n % 2].rearrange("p s l -> p (s l)"),
                        state_in[n % 2].rearrange("p s l -> p (s l)"), 0.0, ALU.mult, ALU.add
                    ).then_inc(scan_done, 1)
                    if n == 1:
                        finish_y(i, 1 - q)
                    if n == PAIRS - 1:
                        dve.wait_ge(du_ready, i + 2)
                    input_of(g + 1, n + 1, q if n < PAIRS - 1 else 1 - q)
                    dve.wait_ge(c_ready, g + 1)
                    dve.wait_ge(scan_done, g + 3)
                    dve.wait_ge(sum_done, g + 1)
                    nc.vector.tensor_tensor(state_c[:, n % 2], states[:, n % 2], c_bank[:],
                                            ALU.mult).then_inc(mul_done, 1)
                    if n == 2:
                        run(stats_of(i + 2, i + 3))
                    if n in (4, 5):
                        next(splitting)
                    if n == 5:
                        dve.wait_ge(out_ready, i + 2)
                        nc.vector.tensor_tensor(x_sb[:, i], x_sb[:, i],
                                                misc.rearrange("p (t d) -> p t d", t=TT),
                                                ALU.add).then_inc(x_added, 1)
                    if n == 6:
                        dve.wait_ge(xt_ready, i + 2)
                        apply_to(i + 2, i + 3)
        yield
        finish_y(BATCH, 1)
        dve.wait_ge(out_ready, BATCH + 2)
        nc.vector.tensor_tensor(x_sb[:, BATCH], x_sb[:, BATCH], misc.rearrange("p (t d) -> p t d", t=TT),
                                ALU.add).then_inc(x_added, 1)
        dve.wait_ge(x_added, BATCH + 2)

    def tensor_program(pe):
        def transpose_xn(r):
            pe.wait_ge(x_added, r)
            pe.wait_ge(xn_ready, TT * (r + 1))
            for t in range(TT):
                last = nc.tensor.transpose(misc[:, t * P:(t + 1) * P], xn[:, t, :], ident[:, :])
            last.then_inc(xt_ready, 1)

        def conv(r, h, taps):
            pe.wait_ge(xt_copied, r + 1)
            for k in taps:
                last = nc.tensor.matmul(front[:, h, :], w_tap[:, h, k, :], x_pad[:, k:k + SEQ],
                                        start=(k == 0), stop=(k == TAPS - 1))
            if TAPS - 1 in taps:
                last.then_inc(conv_ready, 1)

        def project_bc(r, q):
            pe.wait_ge(gated, 2 * r + 1)
            nc.tensor.matmul(front[0:2 * NS, 0, :], w_xp[:, RANK:], u[q][:, :], start=True,
                             stop=True).then_inc(bc_ready, 1)

        def project_delta(r, q):
            nc.tensor.matmul(front[:, 1, :], w_delta[:, :], u[q][:, :], start=True,
                             stop=True).then_inc(dt_ready, 1)

        def spread(dst, i, n, q, c):
            for s in range(2):
                last = nc.tensor.matmul(dst[:, s, :], sel_n[:, c * NS + 2 * n + s, :], bc_parts[q][:, :],
                                        start=True, stop=True)
            return last

        def add_states(g, n):
            pe.wait_ge(pair_added, g + 2)
            nc.tensor.matmul(y_acc, ident[:, :], state_c[:, n % 2, 0, :], start=(n == 0),
                             stop=(n == PAIRS - 1), skip_group_check=True).then_inc(sum_done, 1)

        def project_out(i, q, tiles):
            pe.wait_ge(y_ready, i + 1)
            for t in tiles:
                cols = slice(t * P, (t + 1) * P)
                nc.tensor.matmul(misc[:, cols], y_sb[:, cols], w_out_sb[:, 0, :], start=True, stop=False)
                last = nc.tensor.matmul(misc[:, cols], z[1 - q][:, cols], w_out_sb[:, 1, :], start=False,
                                        stop=True)
            if TT - 1 in tiles:
                last.then_inc(out_ready, 1)

        setup.wait_small(pe)
        pe.wait_ge(setup.taps_done, 2 * TAPS)
        pe.wait_ge(setup.xp_act, 2)
        pe.wait_ge(before_it.sems["w_done"], BATCH * E + 2)
        transpose_xn(0)
        yield
        conv(0, 0, range(TAPS))
        project_bc(0, 0)
        project_delta(0, 0)
        pe.wait_ge(soft_act, 2)
        conv(0, 1, range(TAPS))
        transpose_xn(1)
        pe.wait_ge(parts_ready, 2)
        spread(b_bank, 0, 0, 0, 0).then_inc(b_ready, 1)
        pe.wait_ge(zeroed, 3)
        nc.tensor.matmul(y_acc, ident[:, :], state_c[:, 1, 0, :], start=True, stop=False, skip_group_check=True)
        with pe.Fori(0, BATCH // 2) as turn:
            for q in range(2):
                i = turn * 2 + q
                first = {1: lambda: conv(i + 1, 0, [2]),
                         2: lambda: project_bc(i + 1, 1 - q), 3: lambda: project_out(i, q, [0, 1]),
                         5: lambda: conv(i + 1, 1, [0]), 6: lambda: conv(i + 1, 1, [2]),
                         7: lambda: transpose_xn(i + 2)}
                second = {0: lambda: conv(i + 1, 0, [0, 1]), 1: lambda: conv(i + 1, 0, [3]),
                          2: lambda: project_delta(i + 1, 1 - q), 4: lambda: project_out(i, q, [2, 3]),
                          5: lambda: conv(i + 1, 1, [1]), 6: lambda: conv(i + 1, 1, [3])}
                for n in range(PAIRS):
                    g = i * PAIRS + n
                    pe.wait_ge(in_done, g + 1)
                    if n < PAIRS - 1:
                        spread(b_bank, i, n + 1, q, 0).then_inc(b_ready, 1)
                    else:
                        pe.wait_ge(parts_ready, 2 * (i + 2))
                        spread(b_bank, i, 0, 1 - q, 0).then_inc(b_ready, 1)
                    if n == 3:
                        pe.wait_ge(xt_copied, i + 2)
                    if n == 5:
                        pe.wait_ge(soft_act, (i + 1) * ACT_SOFT + 2)
                    if n in first:
                        first[n]()
                    pe.wait_ge(mul_done, g + 2)
                    spread(c_bank, i, n, q, 1).then_inc(c_ready, 1)
                    if n in second:
                        second[n]()
                    if n == 1:
                        pe.wait_ge(y_ready, i + 1)
                    add_states(g - 1, (n - 1) % PAIRS)
        add_states(BATCH * PAIRS - 1, PAIRS - 1)
        yield
        pe.wait_ge(xt_copied, BATCH + 2)
        project_out(BATCH, 0, range(TT))

    phase.programs = dict(sync=sync_program, gpsimd=gpsimd_program, scalar=scalar_program,
                          vector=vector_program, tensor=tensor_program)
    return phase


_INS = ["L0_attn_hidden_states", "L0_attn_W_in", "L0_attn_W_xproj", "L0_attn_W_dt", "L0_attn_b_dt",
        "L0_attn_A_log", "L0_attn_D", "L0_attn_W_out", "L0_attn_K_x", "L0_attn_b_x", "L0_attn_K_z",
        "L0_attn_b_z", "L0_ffn_router_w", "L0_ffn_bias", "L0_ffn_gate_w", "L0_ffn_up_w", "L0_ffn_down_w",
        "L0_ffn_sh_gate_w", "L0_ffn_sh_up_w", "L0_ffn_sh_down_w"]
_COLUMNS = {"L0_attn_b_dt", "L0_attn_D", "L0_attn_b_x", "L0_attn_b_z"}


def kernel(**inputs):
    import concourse.bacc as _bacc
    from concourse.bass_utils import run_bass_kernel_spmd as _run

    nc = _bacc.Bacc("TRN2", target_bir_lowering=False, num_devices=1)
    arrays, args = {}, []
    for name in _INS:
        a = np.asarray(inputs[name])
        if name in _COLUMNS:
            a = a.reshape(P, 1)
        elif name in ("L0_attn_K_x", "L0_attn_K_z"):
            a = a.reshape(P * TAPS)
        elif name == "L0_ffn_router_w":
            a = a.T
        a = np.ascontiguousarray(a)
        arrays[f"in_{name}"] = a
        args.append(nc.dram_tensor(f"in_{name}", a.shape, mybir.dt.from_np(a.dtype), kind="ExternalInput").ap())
    args.append(nc.dram_tensor("out_0", (BATCH, SEQ, D), FP32, kind="ExternalOutput").ap())
    program(nc, *args)
    r = _run(nc, [arrays], core_ids=[0])
    return r.results[0]["out_0"]
```
